# Optimizing a Trainium2 kernel written in Bass

```python
import numpy as np
import jax
import jax.numpy as jnp

def _softmax(x, axis=-1):
    return jax.nn.softmax(x, axis=axis)

def _gelu(x):
    return jax.nn.gelu(x, approximate=True)

def _silu(x):
    return jax.nn.silu(x)

def _sigmoid(x):
    return jax.nn.sigmoid(x)

def _layernorm(x, axis=-1, eps=1e-05):
    m = jnp.mean(x, axis=axis, keepdims=True)
    v = jnp.var(x, axis=axis, keepdims=True)
    return (x - m) / jnp.sqrt(v + eps)

def _scatter_add(tgt, idx, src, axis=0):
    return tgt.at[idx].add(src)

def _segment_sum(src, seg, n):
    return jax.ops.segment_sum(src, seg, n)
kernel_name = 'mk_cond_resid_d2_seqx_r8_3bb546'

def setup_inputs(seed: int=0):
    np.random.seed(seed)
    _w = jnp.asarray

    def _rec_inputs():
        import jax
        import jax.numpy as jnp
        _rk = jax.random.key(seed)
        x = 7.22e-05 + 1 * jax.random.normal(jax.random.fold_in(_rk, 1), (128, 32, 512), jnp.float32)
        _lenS = 32 - jax.random.randint(jax.random.fold_in(_rk, 7), (128,), 0, max(1, 32 // 4) + 1, jnp.int32)
        _lenS2 = 32 - jax.random.randint(jax.random.fold_in(_rk, 8), (128,), 0, max(1, 32 // 4) + 1, jnp.int32)
        itok_B_2_6 = jax.random.randint(jax.random.fold_in(_rk, 11), (128,), 2, 7, jnp.int32)
        itok_B_0_15 = jax.random.randint(jax.random.fold_in(_rk, 12), (128,), 0, 16, jnp.int32)
        return (x, itok_B_2_6, itok_B_0_15)
    x, itok_B_2_6, itok_B_0_15 = _rec_inputs()

    def _L0_cond_setup():
        import jax, jax.numpy as jnp
        import numpy as np
        B, N, H, F = (4, 64, 512, 1376)
        L, R, RANK = (1, 16, 16)
        SCALE = 0.5
        key = jax.random.key(seed)
        ks = jax.random.split(key, 12)
        nrm = lambda k, shape, fan: jax.random.normal(k, shape, jnp.float32) * fan ** (-0.5)
        inp = {'x': jax.random.normal(ks[0], (B, N, H), jnp.float32), 'W_gate': nrm(ks[1], (F, H), H), 'W_up': nrm(ks[2], (F, H), H), 'W_down': nrm(ks[3], (H, F), F), 'A_gate': nrm(ks[4], (L, R, RANK, H), H), 'B_gate': nrm(ks[5], (L, R, F, RANK), RANK), 'A_up': nrm(ks[6], (L, R, RANK, H), H), 'B_up': nrm(ks[7], (L, R, F, RANK), RANK), 'A_down': nrm(ks[8], (L, R, RANK, F), F), 'B_down': nrm(ks[9], (L, R, H, RANK), RANK), 'lora_indices': jax.random.randint(ks[10], (B,), 0, R), 'layer_idx': 0}
        return inp
    _L0_cond_all = _L0_cond_setup()
    _L0_cond_in = {k: v for k, v in _L0_cond_all.items() if k in ('W_gate', 'W_up', 'W_down', 'A_gate', 'B_gate', 'A_up', 'B_up', 'A_down', 'B_down')}
    del _L0_cond_all

    def _L1_cond_setup():
        import jax, jax.numpy as jnp
        import numpy as np
        B, C, T = (64, 32, 512)
        S, D = (16, 32)
        key = jax.random.key(seed)
        k1, k2, k3 = jax.random.split(key, 3)
        x = jax.random.normal(k1, (B, C, T), dtype=jnp.float32)
        condition = jax.random.randint(k2, (B,), 0, S, dtype=jnp.int64)
        bound = float(np.sqrt(6.0 / C))
        weights = jax.random.uniform(k3, (S, C, D), dtype=jnp.float32, minval=-bound, maxval=bound)
        return {'x': x, 'condition': condition, 'weights': weights}
    _L1_cond_all = _L1_cond_setup()
    _L1_cond_in = {k: v for k, v in _L1_cond_all.items() if k in ('weights',)}
    del _L1_cond_all
    return {'x': x, 'itok_B_2_6': itok_B_2_6, 'itok_B_0_15': itok_B_0_15, 'L0_cond_W_gate': _L0_cond_in['W_gate'], 'L0_cond_W_up': _L0_cond_in['W_up'], 'L0_cond_W_down': _L0_cond_in['W_down'], 'L0_cond_A_gate': _L0_cond_in['A_gate'], 'L0_cond_B_gate': _L0_cond_in['B_gate'], 'L0_cond_A_up': _L0_cond_in['A_up'], 'L0_cond_B_up': _L0_cond_in['B_up'], 'L0_cond_A_down': _L0_cond_in['A_down'], 'L0_cond_B_down': _L0_cond_in['B_down'], 'L1_cond_weights': _L1_cond_in['weights']}

def reference(x, itok_B_2_6, itok_B_0_15, L0_cond_W_gate, L0_cond_W_up, L0_cond_W_down, L0_cond_A_gate, L0_cond_B_gate, L0_cond_A_up, L0_cond_B_up, L0_cond_A_down, L0_cond_B_down, L1_cond_weights):
    import jax
    import jax.numpy as jnp

    def _L0_cond_ref(x, W_gate, W_up, W_down, A_gate, B_gate, A_up, B_up, A_down, B_down, lora_indices, layer_idx):
        import jax, jax.numpy as jnp
        import numpy as np
        B, N, H, F = (4, 64, 512, 1376)
        L, R, RANK = (1, 16, 16)
        SCALE = 0.5

        def lora_add(base, inp, A, B):
            Ab = A[layer_idx][lora_indices]
            Bb = B[layer_idx][lora_indices]
            t = jnp.einsum('bri,bni->bnr', Ab, inp)
            return base + jnp.einsum('bor,bnr->bno', Bb, t) * SCALE
        gate = lora_add(jnp.einsum('bnh,fh->bnf', x, W_gate), x, A_gate, B_gate)
        up = lora_add(jnp.einsum('bnh,fh->bnf', x, W_up), x, A_up, B_up)
        act = jax.nn.silu(gate) * up
        down = lora_add(jnp.einsum('bnf,hf->bnh', act, W_down), act, A_down, B_down)
        return down

    def _L1_cond_ref(x, condition, weights):
        import jax, jax.numpy as jnp
        import numpy as np
        B, C, T = (64, 32, 512)
        S, D = (16, 32)
        W = weights[condition]
        return jnp.einsum('bct,bcd->bdt', x, W)
    x = x + _L0_cond_ref(x, L0_cond_W_gate, L0_cond_W_up, L0_cond_W_down, L0_cond_A_gate, L0_cond_B_gate, L0_cond_A_up, L0_cond_B_up, L0_cond_A_down, L0_cond_B_down, itok_B_2_6, 0)
    x = x + _L1_cond_ref(x, itok_B_0_15, L1_cond_weights)
    return x

_drawn_inputs = setup_inputs


def setup_inputs(seed=0):
    import zlib

    import numpy as np

    out = dict(_drawn_inputs(seed))
    spreads = {}
    factors = {}
    for name, (base, spread) in spreads.items():
        noise = np.random.default_rng([zlib.crc32(name.encode()), seed]).standard_normal(out[name].shape)
        drawn = base * np.exp(spread * noise) if base else spread * noise
        out[name] = jnp.asarray(drawn.astype(out[name].dtype))
    for name, factor in factors.items():
        out[name] = (out[name] * factor).astype(out[name].dtype)
    return out
```

```python
from contextlib import ExitStack

import concourse.bass as bass
from concourse import mybir

F32 = mybir.dt.float32
F32R = mybir.dt.float32r
I32 = mybir.dt.int32
ACT = mybir.ActivationFunctionType
ALU = mybir.AluOpType

P = 128
LORA_SCALE = 0.5


class Tile:

    def __init__(self, pair, offset):
        self.pair, self.offset = pair, offset
        self.parity = offset % 2

    def __add__(self, n):
        return Tile(self.pair, self.offset + n)

    def __sub__(self, n):
        return Tile(self.pair, self.offset - n)

    def times(self, k, plus=0):
        return self.pair * (2 * k) + (k * self.offset + plus)

    def of_parity(self, k):
        return self.pair * k + k * (self.offset // 2 + 1)


def build(nc, x_rows, x_cols, w_gu, w_down, a_all, b_all, w_mix, idx_lora, idx_mix, out):
    TILES, _, H = x_rows.shape
    HC = H // P
    F = w_gu.shape[3]
    SAMPLES = 4
    ROWS = P // SAMPLES
    RANK = b_all.shape[1]
    SR = SAMPLES * RANK
    NS = 3
    W0 = -(-F // (2 * NS)) * 2
    starts = [0, W0, W0 + (F - W0) // 2]
    widths = [W0, (F - W0) // 2, (F - W0) // 2]
    assert sum(widths) == F and all(w % 2 == 0 and w <= 512 for w in widths)
    FC = -(-F // P)
    chunk_rows = [min(P, F - P * k) for k in range(FC)]
    batches = [range(0, starts[1] // P), range(starts[1] // P, starts[2] // P), range(starts[2] // P, FC)]
    BATCH = max(len(b) for b in batches)
    AGU = HC * 2 * RANK
    AD = FC * RANK
    BD0 = 2 * F
    BROW = 2 * F + H
    STAGE = 2 * H
    assert 2 * SR == P and 2 * W0 <= STAGE

    with ExitStack() as ctx:
        def sb(name, shape, dt=F32):
            return ctx.enter_context(nc.sbuf_tensor(name, shape, dt))

        def bank(name):
            return ctx.enter_context(nc.psum_tensor(name, [P, 512], F32))

        def sem(name):
            return ctx.enter_context(nc.semaphore(name))

        wgu_hi = sb("wgu_hi", [P, 2, HC, F], F32R)
        wgu_lo = sb("wgu_lo", [P, 2, HC, F], F32R)
        wd_hi = sb("wd_hi", [P, FC, H], F32R)
        wd_lo = sb("wd_lo", [P, FC, H], F32R)
        stage = sb("stage", [P, 2, STAGE])
        a_raw = sb("a_raw", [P, 2, SAMPLES, AGU + AD])
        agu_hi = sb("agu_hi", [P, SAMPLES, AGU], F32R)
        agu_lo = sb("agu_lo", [P, SAMPLES, AGU], F32R)
        ad_hi = sb("ad_hi", [P, SAMPLES, AD], F32R)
        ad_lo = sb("ad_lo", [P, SAMPLES, AD], F32R)
        b_raw = sb("b_raw", [P, BROW])
        b_gu = sb("b_gu", [P, 2, F], F32R)
        b_dn = sb("b_dn", [P, H], F32R)
        mix_raw = sb("mix_raw", [P, P])
        mix_hi = sb("mix_hi", [P, P], F32R)
        mix_lo = sb("mix_lo", [P, P], F32R)
        xt_raw = sb("xt_raw", [P, HC, P])
        xt_hi = sb("xt_hi", [P, 2, HC, P], F32R)
        xt_lo = sb("xt_lo", [P, 2, HC, P], F32R)
        xr = sb("xr", [P, 2, H])
        h_hi = sb("h_hi", [P, H], F32R)
        h_lo = sb("h_lo", [P, H], F32R)
        act_sb = sb("act_sb", [P, F])
        at_hi = sb("at_hi", [P, 2, BATCH, P], F32R)
        at_lo = sb("at_lo", [P, 2, BATCH, P], F32R)
        t_own = sb("t_own", [P, 2, 2, SR])
        tt_hi = sb("tt_hi", [P, 2, P], F32R)
        tt_lo = sb("tt_lo", [P, 2, P], F32R)
        td_own = sb("td_own", [P, 2, SR])
        tdt_hi = sb("tdt_hi", [P, P], F32R)
        tdt_lo = sb("tdt_lo", [P, P], F32R)
        own = sb("own", [P, SR])
        ident = sb("ident", [P, P])
        idx = sb("idx", [1, 2, idx_lora.shape[0]], I32)

        gu_ps = [bank(f"gu_ps{n}") for n in range(3)]
        d_ps = [bank(f"d_ps{n}") for n in range(2)]
        tr_ps = bank("tr_ps")
        td_ps = bank("td_ps")
        t_bank = bank("t_bank")
        t_ps = t_bank[:, 0:P]
        tt_ps = t_bank[:, P:3 * P].rearrange("p (g n) -> p g n", g=2)
        tdt_ps = t_bank[:, 3 * P:4 * P]

        idx_ld = sem("idx_ld")
        w_ld = [sem(f"w_ld{n}") for n in range(3)]
        xt_ld = sem("xt_ld")
        a_ld = [sem(f"a_ld{n}") for n in range(2)]
        b_ld = [sem(f"b_ld{n}") for n in range(2)]
        mix_ld = sem("mix_ld")
        x_ld = [sem(f"x_ld{n}") for n in range(2)]
        stored = [sem(f"stored{n}") for n in range(2)]
        zeroed = sem("zeroed")
        consts = sem("consts")
        own_zero = sem("own_zero")
        own_set = sem("own_set")
        mix_zero = sem("mix_zero")
        w_hi_done = sem("w_hi_done")
        w_done = sem("w_done")
        xt_hi_done = sem("xt_hi_done")
        xt_done = sem("xt_done")
        agu_hi_done = sem("agu_hi_done")
        agu_done = sem("agu_done")
        ad_hi_done = sem("ad_hi_done")
        ad_done = sem("ad_done")
        b_hi_done = sem("b_hi_done")
        b_done = sem("b_done")
        bd_hi_done = sem("bd_hi_done")
        bd_done = sem("bd_done")
        mix_hi_done = sem("mix_hi_done")
        mix_done = sem("mix_done")
        gate_mm = sem("gate_mm")
        up_mm = sem("up_mm")
        silu_done = sem("silu_done")
        mul_done = sem("mul_done")
        at_mm = sem("at_mm")
        at_hi_done = sem("at_hi_done")
        at_done = sem("at_done")
        dn_mm = sem("dn_mm")
        t_mm = sem("t_mm")
        t_done = sem("t_done")
        tt_mm = sem("tt_mm")
        tt_hi_done = sem("tt_hi_done")
        tt_done = sem("tt_done")
        td_done = sem("td_done")
        tdt_mm = sem("tdt_mm")
        tdt_hi_done = sem("tdt_hi_done")
        tdt_done = sem("tdt_done")
        d_mm = sem("d_mm")
        h_done = sem("h_done")
        h_hi_done = sem("h_hi_done")
        h_split = sem("h_split")
        mix_mm = sem("mix_mm")
        out_done = sem("out_done")

        pieces = []
        for j in range(NS):
            for g in range(2):
                for c in range(0, HC, 2):
                    fs = slice(starts[j], starts[j] + widths[j])
                    pieces.append((wgu_hi[:, g, c:c + 2, fs], wgu_lo[:, g, c:c + 2, fs],
                                   w_gu[g, c:c + 2, :, fs].rearrange("c p f -> p c f"), P, 2, widths[j]))
        GU_PIECES = len(pieces)
        for k in range(0, FC, 2):
            n = min(2, FC - k)
            r = chunk_rows[k] if n == 1 else P
            pieces.append((wd_hi[0:r, k:k + n, :], wd_lo[0:r, k:k + n, :],
                           w_down[k:k + n, 0:r, :].rearrange("c p f -> p c f"), r, n, H))

        def slot(n):
            _, _, _, r, c, w = pieces[n]
            flat = xr[:, :, :].rearrange("p a f -> p (a f)") if n % 3 == 2 else stage[:, n % 3, :]
            return flat[0:r, 0:c * w].rearrange("p (c f) -> p c f", c=c)

        def piece_of(g, j, c):
            return (j * 2 + g) * (HC // 2) + c // 2

        def b_half(tile):
            return (slice(0, SR), slice(SR, P)) if tile.parity == 0 else (slice(SR, P), slice(0, SR))

        def gu_cols(j):
            return slice(starts[j], starts[j] + widths[j])

        block = ctx.enter_context(nc.Block())

        @block.sync
        def _(sp):
            def load_xt(tile, first=False):
                at = sp.snap(tile.times(1))
                if not first:
                    sp.wait_ge(xt_done, tile.times(1))
                sp.dma_start(xt_raw[:], x_cols[bass.ds(at, 1)].rearrange("a p c n -> p (a c) n")
                             ).then_inc(xt_ld, 16)

            def load_a(tile, first=False):
                which = [sp.value_load(idx[0:1, 0, bass.ds(tile.times(SAMPLES, s), 1)], min_val=0,
                                       max_val=a_all.shape[0] - 1) for s in range(SAMPLES)]
                if not first:
                    sp.wait_ge(ad_done, tile.times(1, -1))
                for s in range(SAMPLES):
                    sp.dma_start(a_raw[:, tile.parity, s, :],
                                 a_all[bass.ds(which[s], 1)].rearrange("a p n -> (a p) n")
                                 ).then_inc(a_ld[tile.parity], 16)

            def load_b(tile, first=False):
                which = [sp.value_load(idx[0:1, 0, bass.ds(tile.times(SAMPLES, s), 1)], min_val=0,
                                       max_val=b_all.shape[0] - 1) for s in range(SAMPLES)]
                if not first:
                    sp.wait_ge(bd_done, tile.times(1, -1))
                for s in range(SAMPLES):
                    at = SR * tile.parity + RANK * s
                    sp.dma_start(b_raw[at:at + RANK, :],
                                 b_all[bass.ds(which[s], 1)].rearrange("a r n -> (a r) n")
                                 ).then_inc(b_ld[tile.parity], 16)

            def load_mix(tile, first=False):
                which = [sp.value_load(idx[0:1, 1, bass.ds(tile.times(SAMPLES, s), 1)], min_val=0,
                                       max_val=w_mix.shape[0] - 1) for s in range(SAMPLES)]
                if not first:
                    sp.wait_ge(mix_done, tile.times(1))
                for s in range(SAMPLES):
                    rs = slice(ROWS * s, ROWS * (s + 1))
                    sp.dma_start(mix_raw[rs, rs], w_mix[bass.ds(which[s], 1)].rearrange("a c d -> (a c) d")
                                 ).then_inc(mix_ld, 16)

            def load_x(tile, first=False):
                at = sp.snap(tile.times(1))
                if not first:
                    sp.wait_ge(stored[tile.parity], (tile - 2).of_parity(16))
                sp.dma_start(xr[:, tile.parity, :], x_rows[bass.ds(at, 1)].rearrange("a p h -> (a p) h")
                             ).then_inc(x_ld[tile.parity], 16)

            def store(tile):
                at = sp.snap(tile.times(1))
                sp.wait_ge(out_done, tile.times(1, 1))
                sp.dma_start(out[bass.ds(at, 1)].rearrange("a p h -> (a p) h"), xr[:, tile.parity, :]
                             ).then_inc(stored[tile.parity], 16)

            def load_piece(n):
                if n >= 3:
                    sp.wait_ge(w_done, n - 2)
                sp.dma_start(slot(n), pieces[n][2]).then_inc(w_ld[n % 3], 16)

            sp.dma_start(idx[0:1, 0, :], idx_lora.rearrange("(a n) -> a n", a=1)).then_inc(idx_ld, 16)
            sp.dma_start(idx[0:1, 1, :], idx_mix.rearrange("(a n) -> a n", a=1)).then_inc(idx_ld, 16)
            t0 = Tile(0, 0)
            load_xt(t0, first=True)
            load_piece(0)
            load_piece(1)
            sp.wait_ge(idx_ld, 32)
            load_a(t0, first=True)
            load_piece(2)
            load_piece(3)
            load_b(t0, first=True)
            for n in range(4, 8):
                load_piece(n)
            load_xt(t0 + 1)
            load_a(t0 + 1, first=True)
            for n in range(8, 12):
                load_piece(n)
            load_b(t0 + 1, first=True)
            for n in range(12, len(pieces)):
                load_piece(n)
            sp.wait_ge(mix_zero, 1)
            load_mix(t0, first=True)
            load_xt(t0 + 2)
            sp.wait_ge(w_done, len(pieces))
            load_x(t0, first=True)
            load_a(t0 + 2)
            load_b(t0 + 2)

            def step(i, more=True, head=False):
                if more:
                    load_xt(i + 2)
                load_mix(i)
                if more:
                    load_a(i + 2)
                load_x(i, first=head)
                if more:
                    load_b(i + 2)
                store(i - 1)

            step(t0 + 1, head=True)
            with sp.Fori(1, (TILES - 2) // 2) as pair:
                step(Tile(pair, 0))
                step(Tile(pair, 1))
            step(Tile(0, TILES - 2), more=False)
            step(Tile(0, TILES - 1), more=False)
            last = Tile(0, TILES - 1)
            store(last)
            for tile in (last - 1, last):
                sp.wait_ge(stored[tile.parity], tile.of_parity(16))

        @block.gpsimd
        def _(pool):
            nc.gpsimd.memset(ident[:], 0.0).then_inc(zeroed, 1)
            pool.wait_ge(zeroed, 1)
            nc.gpsimd.affine_select(out=ident[:], in_=ident[:], compare_op=ALU.not_equal, fill=1.0, base=0,
                                    pattern=[[-1, P]], channel_multiplier=1).then_inc(consts, 1)
            nc.gpsimd.memset(mix_raw[:], 0.0).then_inc(mix_zero, 1)

        @block.scalar
        def _(act):
            def hi(dst, src):
                return nc.scalar.activation(dst, src, ACT.Copy)

            def weights(n):
                act.wait_ge(w_ld[n % 3], 16 * (n // 3 + 1))
                hi(pieces[n][0], slot(n)).then_inc(w_hi_done, 1)

            def xt(tile, first=False):
                act.wait_ge(xt_ld, tile.times(16, 16))
                if not first:
                    act.wait_ge(up_mm, tile.times(NS, -NS))
                hi(xt_hi[:, tile.parity], xt_raw[:]).then_inc(xt_hi_done, 1)

            def a_gu(tile, first=False):
                act.wait_ge(a_ld[tile.parity], tile.of_parity(16 * SAMPLES))
                if not first:
                    act.wait_ge(t_mm, tile.times(1))
                hi(agu_hi[:], a_raw[:, tile.parity, :, 0:AGU]).then_inc(agu_hi_done, 1)

            def a_down(tile, first=False):
                act.wait_ge(a_ld[tile.parity], tile.of_parity(16 * SAMPLES))
                if not first:
                    act.wait_ge(dn_mm, tile.times(NS))
                hi(ad_hi[:], a_raw[:, tile.parity, :, AGU:]).then_inc(ad_hi_done, 1)

            def b_slice(tile, j, first=False):
                half, _ = b_half(tile)
                act.wait_ge(b_ld[tile.parity], tile.of_parity(16 * SAMPLES))
                if not first:
                    act.wait_ge(up_mm, tile.times(NS, j + 1 - NS))
                hi(b_gu[half, :, gu_cols(j)],
                   b_raw[half, 0:2 * F].rearrange("p (g f) -> p g f", g=2)[:, :, gu_cols(j)]
                   ).then_inc(b_hi_done, 1)

            def b_down(tile, first=False):
                half, _ = b_half(tile)
                act.wait_ge(b_ld[tile.parity], tile.of_parity(16 * SAMPLES))
                if not first:
                    act.wait_ge(d_mm, tile.times(1))
                hi(b_dn[half, :], b_raw[half, BD0:]).then_inc(bd_hi_done, 1)

            def mix(tile, first=False):
                act.wait_ge(mix_ld, tile.times(16 * SAMPLES, 16 * SAMPLES))
                if not first:
                    act.wait_ge(mix_mm, tile.times(1))
                hi(mix_hi[:], mix_raw[:]).then_inc(mix_hi_done, 1)

            def silu(tile, j, first=False):
                q = tile.times(NS, j)
                act.wait_ge(gate_mm, q + 1)
                if not first:
                    act.wait_ge(at_mm, tile.times(NS, -1 if j == 0 else 0))
                nc.scalar.activation(act_sb[:, gu_cols(j)], gu_ps[(2 * j) % 3][:, 0:widths[j]],
                                     ACT.Silu).then_inc(silu_done, 1)

            def act_t(tile, b, first=False):
                s = (tile.parity * NS + b) % 2
                act.wait_ge(at_mm, tile.times(NS, b + 1))
                if not (first and b < 2):
                    act.wait_ge(dn_mm, tile.times(NS, b - 1))
                n = len(batches[b])
                full = n if chunk_rows[batches[b][-1]] == P else n - 1
                last = hi(at_hi[:, s, 0:full, :], tr_ps[:, 0:full * P].rearrange("p (c n) -> p c n", n=P))
                if full < n:
                    r = chunk_rows[-1]
                    last = hi(at_hi[0:r, s, full, :], tr_ps[0:r, full * P:n * P])
                last.then_inc(at_hi_done, 1)

            def t_t(tile, first=False):
                act.wait_ge(tt_mm, tile.times(1, 1))
                if not first:
                    act.wait_ge(up_mm, tile.times(NS))
                hi(tt_hi[:], tt_ps).then_inc(tt_hi_done, 1)

            def td_t(tile, first=False):
                act.wait_ge(tdt_mm, tile.times(1, 1))
                if not first:
                    act.wait_ge(d_mm, tile.times(1))
                hi(tdt_hi[:], tdt_ps).then_inc(tdt_hi_done, 1)

            def h_part(tile, first=False):
                act.wait_ge(h_done, tile.times(1, 1))
                if not first:
                    act.wait_ge(mix_mm, tile.times(1))
                hi(h_hi[:], xr[:, tile.parity, :]).then_inc(h_hi_done, 1)

            def step(i, prev=True, nxt=True, head=False, second=False):
                if nxt:
                    xt(i + 1, first=head)
                    a_gu(i + 1)
                if prev:
                    mix(i - 1, first=second)
                silu(i, 0, first=head)
                if head:
                    for n in range(8, GU_PIECES):
                        weights(n)
                if prev:
                    act_t(i - 1, 2)
                if nxt:
                    b_slice(i + 1, 0)
                silu(i, 1, first=head)
                if head:
                    for n in range(GU_PIECES, GU_PIECES + 2):
                        weights(n)
                if nxt:
                    b_slice(i + 1, 1)
                act_t(i, 0, first=head)
                a_down(i, first=head)
                if prev:
                    td_t(i - 1, first=second)
                if head:
                    for n in range(GU_PIECES + 2, GU_PIECES + 4):
                        weights(n)
                silu(i, 2, first=head)
                act_t(i, 1, first=head)
                if head:
                    for n in range(GU_PIECES + 4, len(pieces)):
                        weights(n)
                if prev:
                    h_part(i - 1, first=second)
                if nxt:
                    t_t(i + 1)
                    b_slice(i + 1, 2)
                b_down(i, first=head)

            t0 = Tile(0, 0)
            xt(t0, first=True)
            weights(0)
            weights(1)
            a_gu(t0, first=True)
            weights(2)
            weights(3)
            t_t(t0, first=True)
            for j in range(NS):
                b_slice(t0, j, first=True)
            for n in range(4, 8):
                weights(n)
            step(t0, prev=False, head=True)
            step(t0 + 1, second=True)
            with act.Fori(1, (TILES - 2) // 2) as pair:
                step(Tile(pair, 0))
                step(Tile(pair, 1))
            step(Tile(0, TILES - 2))
            step(Tile(0, TILES - 1), nxt=False)
            last = Tile(0, TILES - 1)
            mix(last)
            act_t(last, 2)
            td_t(last)
            h_part(last)

        @block.vector
        def _(dve):
            def lo(dst, src, his):
                return nc.vector.tensor_tensor(dst, src, his.bitcast(F32), ALU.subtract)

            def weights(n):
                dve.wait_ge(w_hi_done, n + 1)
                lo(pieces[n][1], slot(n), pieces[n][0]).then_inc(w_done, 1)

            def xt(tile):
                dve.wait_ge(xt_hi_done, tile.times(1, 1))
                lo(xt_lo[:, tile.parity], xt_raw[:], xt_hi[:, tile.parity]).then_inc(xt_done, 1)

            def a_gu(tile):
                dve.wait_ge(agu_hi_done, tile.times(1, 1))
                lo(agu_lo[:], a_raw[:, tile.parity, :, 0:AGU], agu_hi[:]).then_inc(agu_done, 1)

            def a_down(tile):
                dve.wait_ge(ad_hi_done, tile.times(1, 1))
                lo(ad_lo[:], a_raw[:, tile.parity, :, AGU:], ad_hi[:]).then_inc(ad_done, 1)

            def b_slice(tile, j):
                half, other = b_half(tile)
                dve.wait_ge(b_hi_done, tile.times(NS, j + 1))
                lo(b_gu[other, :, gu_cols(j)],
                   b_raw[half, 0:2 * F].rearrange("p (g f) -> p g f", g=2)[:, :, gu_cols(j)],
                   b_gu[half, :, gu_cols(j)]).then_inc(b_done, 1)

            def b_down(tile):
                half, other = b_half(tile)
                dve.wait_ge(bd_hi_done, tile.times(1, 1))
                lo(b_dn[other, :], b_raw[half, BD0:], b_dn[half, :]).then_inc(bd_done, 1)

            def mix(tile):
                dve.wait_ge(mix_hi_done, tile.times(1, 1))
                lo(mix_lo[:], mix_raw[:], mix_hi[:]).then_inc(mix_done, 1)

            def mul(tile, j):
                dve.wait_ge(silu_done, tile.times(NS, j + 1))
                dve.wait_ge(up_mm, tile.times(NS, j + 1))
                s = act_sb[:, gu_cols(j)]
                nc.vector.tensor_tensor(s, gu_ps[(2 * j + 1) % 3][:, 0:widths[j]], s, ALU.mult
                                        ).then_inc(mul_done, 1)

            def act_t(tile, b):
                s = (tile.parity * NS + b) % 2
                dve.wait_ge(at_hi_done, tile.times(NS, b + 1))
                n = len(batches[b])
                full = n if chunk_rows[batches[b][-1]] == P else n - 1
                last = lo(at_lo[:, s, 0:full, :], tr_ps[:, 0:full * P].rearrange("p (c n) -> p c n", n=P),
                          at_hi[:, s, 0:full, :])
                if full < n:
                    r = chunk_rows[-1]
                    last = lo(at_lo[0:r, s, full, :], tr_ps[0:r, full * P:n * P], at_hi[0:r, s, full, :])
                last.then_inc(at_done, 1)

            def t_mask(tile, first=False):
                dve.wait_ge(t_mm, tile.times(1, 1))
                if not first:
                    dve.wait_ge(tt_mm, tile.times(1))
                for g in range(2):
                    src = t_ps.rearrange("p (s g r) -> p g s r", g=2, r=RANK)[:, g]
                    for d in range(2):
                        last = nc.vector.tensor_tensor(
                            t_own[:, g, d, :].rearrange("p (s r) -> p s r", r=RANK), src,
                            own[:].rearrange("p (s r) -> p s r", r=RANK), ALU.mult)
                last.then_inc(t_done, 1)

            def td_mask(tile, first=False):
                dve.wait_ge(dn_mm, tile.times(NS, NS))
                if not first:
                    dve.wait_ge(tdt_mm, tile.times(1))
                for d in range(2):
                    last = nc.vector.tensor_tensor(td_own[:, d, :], td_ps[:, 0:SR], own[:], ALU.mult)
                last.then_inc(td_done, 1)

            def t_t(tile):
                dve.wait_ge(tt_hi_done, tile.times(1, 1))
                lo(tt_lo[:], tt_ps, tt_hi[:]).then_inc(tt_done, 1)

            def td_t(tile):
                dve.wait_ge(tdt_hi_done, tile.times(1, 1))
                lo(tdt_lo[:], tdt_ps, tdt_hi[:]).then_inc(tdt_done, 1)

            def h_sum(tile):
                dve.wait_ge(d_mm, tile.times(1, 1))
                dve.wait_ge(x_ld[tile.parity], tile.of_parity(16))
                nc.vector.tensor_tensor(xr[:, tile.parity, :], d_ps[tile.parity][:, 0:H], xr[:, tile.parity, :],
                                        ALU.add).then_inc(h_done, 1)

            def h_part(tile):
                dve.wait_ge(h_hi_done, tile.times(1, 1))
                lo(h_lo[:], xr[:, tile.parity, :], h_hi[:]).then_inc(h_split, 1)

            def out_sum(tile):
                dve.wait_ge(mix_mm, tile.times(1, 1))
                nc.vector.tensor_tensor(xr[:, tile.parity, :], d_ps[tile.parity][:, 0:H], xr[:, tile.parity, :],
                                        ALU.add).then_inc(out_done, 1)

            def step(i, prev=True, nxt=True, head=False, second=False):
                if nxt:
                    xt(i + 1)
                    a_gu(i + 1)
                if prev:
                    mix(i - 1)
                mul(i, 0)
                if head:
                    for n in range(8, GU_PIECES):
                        weights(n)
                if prev:
                    act_t(i - 1, 2)
                if nxt:
                    t_mask(i + 1)
                    b_slice(i + 1, 0)
                mul(i, 1)
                if head:
                    for n in range(GU_PIECES, GU_PIECES + 2):
                        weights(n)
                if nxt:
                    b_slice(i + 1, 1)
                if prev:
                    td_mask(i - 1, first=second)
                act_t(i, 0)
                a_down(i)
                if prev:
                    td_t(i - 1)
                if head:
                    for n in range(GU_PIECES + 2, GU_PIECES + 4):
                        weights(n)
                if prev:
                    h_sum(i - 1)
                act_t(i, 1)
                if head:
                    for n in range(GU_PIECES + 4, len(pieces)):
                        weights(n)
                if prev:
                    h_part(i - 1)
                mul(i, 2)
                if nxt:
                    t_t(i + 1)
                    b_slice(i + 1, 2)
                b_down(i)
                if prev:
                    out_sum(i - 1)

            nc.vector.memset(own[:], 0.0).then_inc(own_zero, 1)
            dve.wait_ge(own_zero, 1)
            for s in range(SAMPLES):
                nc.vector.memset(own[ROWS * s:ROWS * (s + 1), RANK * s:RANK * (s + 1)], LORA_SCALE
                                 ).then_inc(own_set, 1)
            dve.wait_ge(own_set, SAMPLES)
            t0 = Tile(0, 0)
            xt(t0)
            weights(0)
            weights(1)
            a_gu(t0)
            t_mask(t0, first=True)
            weights(2)
            weights(3)
            t_t(t0)
            for j in range(NS):
                b_slice(t0, j)
            for n in range(4, 8):
                weights(n)
            step(t0, prev=False, head=True)
            step(t0 + 1, second=True)
            with dve.Fori(1, (TILES - 2) // 2) as pair:
                step(Tile(pair, 0))
                step(Tile(pair, 1))
            step(Tile(0, TILES - 2))
            step(Tile(0, TILES - 1), nxt=False)
            last = Tile(0, TILES - 1)
            mix(last)
            act_t(last, 2)
            td_mask(last)
            td_t(last)
            h_sum(last)
            h_part(last)
            out_sum(last)

        @block.tensor
        def _(pe):
            def t_product(tile, first=False):
                pe.wait_ge(xt_done, tile.times(1, 1))
                pe.wait_ge(agu_done, tile.times(1, 1))
                if not first:
                    pe.wait_ge(t_done, tile.times(1))
                p = tile.parity
                for c in range(HC):
                    a_hi = agu_hi[:, :, 2 * RANK * c:2 * RANK * (c + 1)]
                    a_lo = agu_lo[:, :, 2 * RANK * c:2 * RANK * (c + 1)]
                    nc.tensor.matmul(t_ps, xt_hi[:, p, c, :], a_hi, start=(c == 0), stop=False)
                    nc.tensor.matmul(t_ps, xt_hi[:, p, c, :], a_lo, start=False, stop=False)
                    last = nc.tensor.matmul(t_ps, xt_lo[:, p, c, :], a_hi, start=False, stop=(c == HC - 1))
                last.then_inc(t_mm, 1)

            def t_transpose(tile, first=False):
                pe.wait_ge(t_done, tile.times(1, 1))
                if not first:
                    pe.wait_ge(tt_done, tile.times(1))
                for g in range(2):
                    last = nc.tensor.transpose(tt_ps[:, g, :], t_own[:, g].rearrange("p d n -> p (d n)"),
                                               ident[:])
                last.then_inc(tt_mm, 1)

            def dense(tile, j, g, head=False):
                if g == 0:
                    if not (head and j < 2):
                        pe.wait_ge(mul_done, tile.times(NS, j - 1))
                elif not (head and j == 0):
                    pe.wait_ge(silu_done, tile.times(NS, j))
                ps = gu_ps[(2 * j + g) % 3][:, 0:widths[j]]
                p = tile.parity
                for c in range(HC):
                    if head and c % 2 == 0:
                        pe.wait_ge(w_done, piece_of(g, j, c) + 1)
                    w_hi, w_lo = wgu_hi[:, g, c, gu_cols(j)], wgu_lo[:, g, c, gu_cols(j)]
                    nc.tensor.matmul(ps, xt_hi[:, p, c, :], w_hi, start=(c == 0), stop=False)
                    nc.tensor.matmul(ps, xt_hi[:, p, c, :], w_lo, start=False, stop=False)
                    nc.tensor.matmul(ps, xt_lo[:, p, c, :], w_hi, start=False, stop=False)

            def adapt(tile, j):
                pe.wait_ge(tt_done, tile.times(1, 1))
                pe.wait_ge(b_done, tile.times(NS, j + 1))
                for g, done in ((0, gate_mm), (1, up_mm)):
                    ps = gu_ps[(2 * j + g) % 3][:, 0:widths[j]]
                    nc.tensor.matmul(ps, tt_hi[:, g, :], b_gu[:, g, gu_cols(j)], start=False, stop=False)
                    nc.tensor.matmul(ps, tt_lo[:, g, :], b_gu[:, g, gu_cols(j)], start=False, stop=True
                                     ).then_inc(done, 1)

            def act_transpose(tile, b, head=False):
                pe.wait_ge(mul_done, tile.times(NS, b + 1))
                if not (head and b == 0):
                    pe.wait_ge(at_done, tile.times(NS, b))
                for n, k in enumerate(batches[b]):
                    r = chunk_rows[k]
                    last = nc.tensor.transpose(tr_ps[0:r, P * n:P * (n + 1)], act_sb[:, P * k:P * k + r],
                                               ident[:])
                last.then_inc(at_mm, 1)

            def down(tile, b, head=False, second=False):
                p, s = tile.parity, (tile.parity * NS + b) % 2
                pe.wait_ge(at_done, tile.times(NS, b + 1))
                if b == 0:
                    pe.wait_ge(ad_done, tile.times(1, 1))
                    if not head:
                        pe.wait_ge(td_done, tile.times(1))
                    if not (head or second):
                        pe.wait_ge(out_done, tile.times(1, -1))
                for n, k in enumerate(batches[b]):
                    if head:
                        pe.wait_ge(w_done, GU_PIECES + k // 2 + 1)
                    r = chunk_rows[k]
                    a_hi, a_lo = at_hi[0:r, s, n, :], at_lo[0:r, s, n, :]
                    d_hi = ad_hi[0:r, :, RANK * k:RANK * (k + 1)]
                    d_lo = ad_lo[0:r, :, RANK * k:RANK * (k + 1)]
                    dp, tp = d_ps[p][:, 0:H], td_ps[:, 0:SR]
                    nc.tensor.matmul(dp, a_hi, wd_hi[0:r, k, :], start=(k == 0), stop=False)
                    nc.tensor.matmul(dp, a_hi, wd_lo[0:r, k, :], start=False, stop=False)
                    nc.tensor.matmul(tp, a_hi, d_hi, start=(k == 0), stop=False)
                    nc.tensor.matmul(tp, a_hi, d_lo, start=False, stop=False)
                    nc.tensor.matmul(tp, a_lo, d_hi, start=False, stop=(k == FC - 1))
                    last = nc.tensor.matmul(dp, a_lo, wd_hi[0:r, k, :], start=False, stop=False)
                last.then_inc(dn_mm, 1)

            def td_transpose(tile):
                pe.wait_ge(td_done, tile.times(1, 1))
                nc.tensor.transpose(tdt_ps, td_own[:].rearrange("p d n -> p (d n)"), ident[:]
                                    ).then_inc(tdt_mm, 1)

            def adapt_down(tile):
                pe.wait_ge(tdt_done, tile.times(1, 1))
                pe.wait_ge(bd_done, tile.times(1, 1))
                ps = d_ps[tile.parity][:, 0:H]
                nc.tensor.matmul(ps, tdt_hi[:], b_dn[:], start=False, stop=False)
                nc.tensor.matmul(ps, tdt_lo[:], b_dn[:], start=False, stop=True).then_inc(d_mm, 1)

            def mix(tile):
                pe.wait_ge(mix_done, tile.times(1, 1))
                pe.wait_ge(h_split, tile.times(1, 1))
                ps = d_ps[tile.parity][:, 0:H]
                nc.tensor.matmul(ps, mix_hi[:], h_hi[:], start=True, stop=False)
                nc.tensor.matmul(ps, mix_lo[:], h_hi[:], start=False, stop=False)
                nc.tensor.matmul(ps, mix_hi[:], h_lo[:], start=False, stop=True).then_inc(mix_mm, 1)

            def step(i, prev=True, nxt=True, head=False, second=False):
                dense(i, 0, 0, head=head)
                dense(i, 0, 1, head=head)
                adapt(i, 0)
                if prev:
                    act_transpose(i - 1, 2)
                if nxt:
                    t_product(i + 1)
                dense(i, 1, 0, head=head)
                dense(i, 1, 1, head=head)
                adapt(i, 1)
                if prev:
                    down(i - 1, 2, head=second)
                act_transpose(i, 0, head=head)
                if nxt:
                    t_transpose(i + 1)
                dense(i, 2, 0, head=head)
                if prev:
                    td_transpose(i - 1)
                dense(i, 2, 1, head=head)
                adapt(i, 2)
                if prev:
                    adapt_down(i - 1)
                act_transpose(i, 1, head=head)
                down(i, 0, head=head, second=second)
                if prev:
                    mix(i - 1)
                down(i, 1, head=head)

            t0 = Tile(0, 0)
            pe.wait_ge(consts, 1)
            t_product(t0, first=True)
            t_transpose(t0, first=True)
            step(t0, prev=False, head=True)
            step(t0 + 1, second=True)
            with pe.Fori(1, (TILES - 2) // 2) as pair:
                step(Tile(pair, 0))
                step(Tile(pair, 1))
            step(Tile(0, TILES - 2))
            step(Tile(0, TILES - 1), nxt=False)
            last = Tile(0, TILES - 1)
            act_transpose(last, 2)
            down(last, 2)
            td_transpose(last)
            adapt_down(last)
            mix(last)


def kernel(**inputs):
    import numpy as np
    import concourse.bacc as bacc
    from concourse.bass_utils import run_bass_kernel_spmd

    given = {k: np.asarray(v) for k, v in inputs.items()}
    x = given["x"]
    rows, hidden = x.shape[0] * x.shape[1], x.shape[2]
    tiles, hc = rows // P, hidden // P
    wg, wu, wd = (given[f"L0_cond_W_{n}"] for n in ("gate", "up", "down"))
    f = wg.shape[0]
    fc = -(-f // P)

    def by_partition(a):
        a = np.pad(a, ((0, 0), (0, 0), (0, -a.shape[2] % P)))
        return a.reshape(a.shape[0], a.shape[1], -1, P).transpose(0, 3, 2, 1)

    ag, au, ad = (given[f"L0_cond_A_{n}"][0] for n in ("gate", "up", "down"))
    bg, bu, bd = (given[f"L0_cond_B_{n}"][0] for n in ("gate", "up", "down"))
    n_adapters = ag.shape[0]
    a_gu = np.stack([by_partition(ag), by_partition(au)], axis=3)
    a_all = np.concatenate([a_gu.reshape(n_adapters, P, -1), by_partition(ad).reshape(n_adapters, P, -1)],
                           axis=2)
    b_all = np.concatenate([b.transpose(0, 2, 1) for b in (bg, bu, bd)], axis=2)
    arrays = {
        "x_rows": x.reshape(tiles, P, hidden),
        "x_cols": x.reshape(tiles, P, hc, P).transpose(0, 3, 2, 1),
        "w_gu": np.stack([w.T.reshape(hc, P, f) for w in (wg, wu)]),
        "w_down": np.pad(wd.T, ((0, fc * P - f), (0, 0))).reshape(fc, P, hidden),
        "a_all": a_all,
        "b_all": b_all,
        "w_mix": given["L1_cond_weights"],
        "idx_lora": given["itok_B_2_6"],
        "idx_mix": given["itok_B_0_15"],
    }
    arrays = {k: np.ascontiguousarray(v) for k, v in arrays.items()}
    nc = bacc.Bacc("TRN2", target_bir_lowering=False, num_devices=1, dynamic_dma_scratch_size=1024)
    args = [nc.dram_tensor(f"in_{k}", v.shape, mybir.dt.from_np(v.dtype), kind="ExternalInput").ap()
            for k, v in arrays.items()]
    out = nc.dram_tensor("out_0", (tiles, P, hidden), F32, kind="ExternalOutput").ap()
    build(nc, *args, out)
    r = run_bass_kernel_spmd(nc, [{f"in_{k}": v for k, v in arrays.items()}], core_ids=[0])
    return r.results[0]["out_0"].reshape(x.shape)
```

```python
from contextlib import ExitStack

import concourse.bass as bass
from concourse import mybir

F32 = mybir.dt.float32
F32R = mybir.dt.float32r
I32 = mybir.dt.int32
ACT = mybir.ActivationFunctionType
ALU = mybir.AluOpType

P = 128
LORA_SCALE = 0.5


class Tile:

    def __init__(self, pair, offset):
        self.pair, self.offset = pair, offset
        self.parity = offset % 2

    def __add__(self, n):
        return Tile(self.pair, self.offset + n)

    def __sub__(self, n):
        return Tile(self.pair, self.offset - n)

    def times(self, k, plus=0):
        return self.pair * (2 * k) + (k * self.offset + plus)

    def of_parity(self, k):
        return self.pair * k + k * (self.offset // 2 + 1)


def build(nc, x_rows, x_cols, w_gu, w_down, a_all, b_all, w_mix, idx_lora, idx_mix, out):
    TILES, _, H = x_rows.shape
    HC = H // P
    F = w_gu.shape[3]
    SAMPLES = 4
    ROWS = P // SAMPLES
    RANK = b_all.shape[1]
    SR = SAMPLES * RANK
    NS = 3
    SW = (SR + F) // NS
    starts = [max(0, SW * j - SR) for j in range(NS)]
    widths = [SW * (j + 1) - SR - starts[j] for j in range(NS)]
    assert NS * SW == SR + F and SW % 2 == 0 and SW <= 512
    FC = -(-F // P)
    chunk_rows = [min(P, F - P * k) for k in range(FC)]
    batches = [range(0, starts[1] // P), range(starts[1] // P, starts[2] // P), range(starts[2] // P, FC)]
    BATCH = max(len(b) for b in batches)
    AGU = HC * 2 * RANK
    AD = FC * RANK
    BD0 = 2 * F
    BROW = 2 * F + H
    STAGE = 2 * H
    HH = H // 2
    assert 2 * SR == P and 2 * max(widths) <= STAGE and HH + SR <= 512

    with ExitStack() as ctx:
        def sb(name, shape, dt=F32):
            return ctx.enter_context(nc.sbuf_tensor(name, shape, dt))

        def bank(name):
            return ctx.enter_context(nc.psum_tensor(name, [P, 512], F32))

        def sem(name):
            return ctx.enter_context(nc.semaphore(name))

        wgu_hi = sb("wgu_hi", [P, 2, HC, SR + F], F32R)
        wgu_lo = sb("wgu_lo", [P, 2, HC, SR + F], F32R)
        wd_hi = sb("wd_hi", [P, FC, H + SR], F32R)
        wd_lo = sb("wd_lo", [P, FC, H + SR], F32R)
        stage = sb("stage", [P, 2, STAGE])
        a_raw = sb("a_raw", [P, 2, SAMPLES, AGU + AD])
        b_raw = sb("b_raw", [P, BROW])
        b_gu = sb("b_gu", [P, 2, F], F32R)
        b_dn = sb("b_dn", [P, H], F32R)
        mix_raw = sb("mix_raw", [P, P])
        mix_hi = sb("mix_hi", [P, P], F32R)
        mix_lo = sb("mix_lo", [P, P], F32R)
        xt_raw = sb("xt_raw", [P, HC, P])
        xt_hi = sb("xt_hi", [P, 2, HC, P], F32R)
        xt_lo = sb("xt_lo", [P, 2, HC, P], F32R)
        xr = sb("xr", [P, 2, H])
        h_hi = sb("h_hi", [P, H], F32R)
        h_lo = sb("h_lo", [P, H], F32R)
        act_sb = sb("act_sb", [P, F])
        at_hi = sb("at_hi", [P, 2, BATCH, P], F32R)
        at_lo = sb("at_lo", [P, 2, BATCH, P], F32R)
        t_own = sb("t_own", [P, 2, 2, SR])
        tt_hi = sb("tt_hi", [P, 2, P], F32R)
        tt_lo = sb("tt_lo", [P, 2, P], F32R)
        td_own = sb("td_own", [P, 2, SR])
        tdt_hi = sb("tdt_hi", [P, P], F32R)
        tdt_lo = sb("tdt_lo", [P, P], F32R)
        own = sb("own", [P, SR])
        ident = sb("ident", [P, P])
        idx = sb("idx", [1, 2, idx_lora.shape[0]], I32)

        gu_ps = [bank(f"gu_ps{n}") for n in range(3)]
        d_banks = ctx.enter_context(nc.psum_tensor("d_banks", [P, 2, 512], F32))
        d_ps = d_banks[:, :, 0:HH]
        td_ps = d_banks[:, 1, HH:HH + SR]
        mix_ps = bank("mix_ps")[:, 0:H]
        tr_ps = bank("tr_ps")
        t_bank = bank("t_bank")
        tt_ps = t_bank[:, 0:2 * P].rearrange("p (g n) -> p g n", g=2)
        tdt_ps = t_bank[:, 2 * P:3 * P]

        idx_ld = sem("idx_ld")
        w_ld = [sem(f"w_ld{n}") for n in range(3)]
        xt_ld = sem("xt_ld")
        a_ld = [sem(f"a_ld{n}") for n in range(2)]
        b_ld = [sem(f"b_ld{n}") for n in range(2)]
        mix_ld = sem("mix_ld")
        x_ld = [sem(f"x_ld{n}") for n in range(2)]
        stored = [sem(f"stored{n}") for n in range(2)]
        zeroed = sem("zeroed")
        consts = sem("consts")
        own_zero = sem("own_zero")
        own_set = sem("own_set")
        mix_zero = sem("mix_zero")
        w_hi_done = sem("w_hi_done")
        w_done = sem("w_done")
        xt_hi_done = sem("xt_hi_done")
        xt_done = sem("xt_done")
        agu_hi_done = sem("agu_hi_done")
        agu_done = sem("agu_done")
        ad_hi_done = sem("ad_hi_done")
        ad_done = sem("ad_done")
        b_hi_done = sem("b_hi_done")
        b_done = sem("b_done")
        bd_hi_done = sem("bd_hi_done")
        bd_done = sem("bd_done")
        mix_hi_done = sem("mix_hi_done")
        mix_done = sem("mix_done")
        gate_mm = sem("gate_mm")
        up_mm = sem("up_mm")
        silu_done = sem("silu_done")
        mul_done = sem("mul_done")
        at_mm = sem("at_mm")
        at_hi_done = sem("at_hi_done")
        at_done = sem("at_done")
        dn_mm = sem("dn_mm")
        t_mm = sem("t_mm")
        t_done = sem("t_done")
        tt_mm = sem("tt_mm")
        tt_hi_done = sem("tt_hi_done")
        tt_done = sem("tt_done")
        td_done = sem("td_done")
        tdt_mm = sem("tdt_mm")
        tdt_hi_done = sem("tdt_hi_done")
        tdt_done = sem("tdt_done")
        d_mm = sem("d_mm")
        h_done = sem("h_done")
        h_hi_done = sem("h_hi_done")
        h_split = sem("h_split")
        mix_mm = sem("mix_mm")
        out_done = sem("out_done")

        pieces = []
        for j in range(NS):
            for g in range(2):
                for c in range(0, HC, 2):
                    fs = slice(starts[j], starts[j] + widths[j])
                    ws = slice(SR + starts[j], SR + starts[j] + widths[j])
                    pieces.append((wgu_hi[:, g, c:c + 2, ws], wgu_lo[:, g, c:c + 2, ws],
                                   w_gu[g, c:c + 2, :, fs].rearrange("c p f -> p c f"), P, 2, widths[j]))
        GU_PIECES = len(pieces)
        for k in range(0, FC, 2):
            n = min(2, FC - k)
            r = chunk_rows[k] if n == 1 else P
            pieces.append((wd_hi[0:r, k:k + n, 0:H], wd_lo[0:r, k:k + n, 0:H],
                           w_down[k:k + n, 0:r, :].rearrange("c p f -> p c f"), r, n, H))

        def slot(n):
            _, _, _, r, c, w = pieces[n]
            flat = xr[:, :, :].rearrange("p a f -> p (a f)") if n % 3 == 2 else stage[:, n % 3, :]
            return flat[0:r, 0:c * w].rearrange("p (c f) -> p c f", c=c)

        def piece_of(g, j, c):
            return (j * 2 + g) * (HC // 2) + c // 2

        def b_half(tile):
            return (slice(0, SR), slice(SR, P)) if tile.parity == 0 else (slice(SR, P), slice(0, SR))

        def gu_cols(j):
            return slice(starts[j], starts[j] + widths[j])

        def gu_out(j, g):
            return gu_ps[(2 * j + g) % 3][:, SW - widths[j]:SW]

        def a_gu_to(w):
            return w[:, :, :, 0:SR].rearrange("p g c (s r) -> p s (g c) r", s=SAMPLES)

        def a_gu_from(tile):
            return a_raw[:, tile.parity, :, 0:AGU].rearrange("p s (n r) -> p s n r", r=RANK)

        def a_down_to(w):
            return w[:, :, H:].rearrange("p k (s r) -> p s k r", s=SAMPLES)

        def a_down_from(tile):
            return a_raw[:, tile.parity, :, AGU:].rearrange("p s (k r) -> p s k r", r=RANK)

        block = ctx.enter_context(nc.Block())

        @block.sync
        def _(sp):
            def load_xt(tile, first=False):
                at = sp.snap(tile.times(1))
                if not first:
                    sp.wait_ge(xt_done, tile.times(1))
                sp.dma_start(xt_raw[:], x_cols[bass.ds(at, 1)].rearrange("a p c n -> p (a c) n")
                             ).then_inc(xt_ld, 16)

            def load_a(tile, first=False):
                which = [sp.value_load(idx[0:1, 0, bass.ds(tile.times(SAMPLES, s), 1)], min_val=0,
                                       max_val=a_all.shape[0] - 1) for s in range(SAMPLES)]
                if not first:
                    sp.wait_ge(ad_done, tile.times(1, -1))
                for s in range(SAMPLES):
                    sp.dma_start(a_raw[:, tile.parity, s, :],
                                 a_all[bass.ds(which[s], 1)].rearrange("a p n -> (a p) n")
                                 ).then_inc(a_ld[tile.parity], 16)

            def load_b(tile, first=False):
                which = [sp.value_load(idx[0:1, 0, bass.ds(tile.times(SAMPLES, s), 1)], min_val=0,
                                       max_val=b_all.shape[0] - 1) for s in range(SAMPLES)]
                if not first:
                    sp.wait_ge(bd_done, tile.times(1, -1))
                for s in range(SAMPLES):
                    at = SR * tile.parity + RANK * s
                    sp.dma_start(b_raw[at:at + RANK, :],
                                 b_all[bass.ds(which[s], 1)].rearrange("a r n -> (a r) n")
                                 ).then_inc(b_ld[tile.parity], 16)

            def load_mix(tile, first=False):
                which = [sp.value_load(idx[0:1, 1, bass.ds(tile.times(SAMPLES, s), 1)], min_val=0,
                                       max_val=w_mix.shape[0] - 1) for s in range(SAMPLES)]
                if not first:
                    sp.wait_ge(mix_done, tile.times(1))
                for s in range(SAMPLES):
                    rs = slice(ROWS * s, ROWS * (s + 1))
                    sp.dma_start(mix_raw[rs, rs], w_mix[bass.ds(which[s], 1)].rearrange("a c d -> (a c) d")
                                 ).then_inc(mix_ld, 16)

            def load_x(tile, first=False):
                at = sp.snap(tile.times(1))
                if not first:
                    sp.wait_ge(stored[tile.parity], (tile - 2).of_parity(16))
                sp.dma_start(xr[:, tile.parity, :], x_rows[bass.ds(at, 1)].rearrange("a p h -> (a p) h")
                             ).then_inc(x_ld[tile.parity], 16)

            def store(tile):
                at = sp.snap(tile.times(1))
                sp.wait_ge(out_done, tile.times(1, 1))
                sp.dma_start(out[bass.ds(at, 1)].rearrange("a p h -> (a p) h"), xr[:, tile.parity, :]
                             ).then_inc(stored[tile.parity], 16)

            def load_piece(n):
                if n >= 3:
                    sp.wait_ge(w_done, n - 2)
                sp.dma_start(slot(n), pieces[n][2]).then_inc(w_ld[n % 3], 16)

            sp.dma_start(idx[0:1, 0, :], idx_lora.rearrange("(a n) -> a n", a=1)).then_inc(idx_ld, 16)
            sp.dma_start(idx[0:1, 1, :], idx_mix.rearrange("(a n) -> a n", a=1)).then_inc(idx_ld, 16)
            t0 = Tile(0, 0)
            load_xt(t0, first=True)
            sp.wait_ge(idx_ld, 32)
            load_a(t0, first=True)
            for n in range(0, 6):
                load_piece(n)
            load_b(t0, first=True)
            for n in range(6, 8):
                load_piece(n)
            load_xt(t0 + 1)
            load_a(t0 + 1, first=True)
            for n in range(8, 12):
                load_piece(n)
            load_b(t0 + 1, first=True)
            for n in range(12, len(pieces)):
                load_piece(n)
            sp.wait_ge(mix_zero, 1)
            load_mix(t0, first=True)
            load_xt(t0 + 2)
            sp.wait_ge(w_done, len(pieces))
            load_x(t0, first=True)
            load_a(t0 + 2)
            load_b(t0 + 2)

            def step(i, more=True, head=False):
                if more:
                    load_xt(i + 2)
                load_mix(i)
                if more:
                    load_a(i + 2)
                load_x(i, first=head)
                if more:
                    load_b(i + 2)
                store(i - 1)

            step(t0 + 1, head=True)
            with sp.Fori(1, (TILES - 2) // 2) as pair:
                step(Tile(pair, 0))
                step(Tile(pair, 1))
            step(Tile(0, TILES - 2), more=False)
            step(Tile(0, TILES - 1), more=False)
            last = Tile(0, TILES - 1)
            store(last)
            for tile in (last - 1, last):
                sp.wait_ge(stored[tile.parity], tile.of_parity(16))

        @block.gpsimd
        def _(pool):
            nc.gpsimd.memset(ident[:], 0.0).then_inc(zeroed, 1)
            pool.wait_ge(zeroed, 1)
            nc.gpsimd.affine_select(out=ident[:], in_=ident[:], compare_op=ALU.not_equal, fill=1.0, base=0,
                                    pattern=[[-1, P]], channel_multiplier=1).then_inc(consts, 1)
            nc.gpsimd.memset(mix_raw[:], 0.0).then_inc(mix_zero, 1)

        @block.scalar
        def _(act):
            def hi(dst, src):
                return nc.scalar.activation(dst, src, ACT.Copy)

            def weights(n):
                act.wait_ge(w_ld[n % 3], 16 * (n // 3 + 1))
                hi(pieces[n][0], slot(n)).then_inc(w_hi_done, 1)

            def xt(tile, first=False):
                act.wait_ge(xt_ld, tile.times(16, 16))
                if not first:
                    act.wait_ge(up_mm, tile.times(NS, -NS))
                hi(xt_hi[:, tile.parity], xt_raw[:]).then_inc(xt_hi_done, 1)

            def a_gu(tile, first=False):
                act.wait_ge(a_ld[tile.parity], tile.of_parity(16 * SAMPLES))
                if not first:
                    act.wait_ge(t_mm, tile.times(1))
                hi(a_gu_to(wgu_hi), a_gu_from(tile)).then_inc(agu_hi_done, 1)

            def a_down(tile, first=False):
                act.wait_ge(a_ld[tile.parity], tile.of_parity(16 * SAMPLES))
                if not first:
                    act.wait_ge(dn_mm, tile.times(NS))
                hi(a_down_to(wd_hi), a_down_from(tile)).then_inc(ad_hi_done, 1)

            def b_slice(tile, j, first=False):
                half, _ = b_half(tile)
                act.wait_ge(b_ld[tile.parity], tile.of_parity(16 * SAMPLES))
                if not first:
                    act.wait_ge(up_mm, tile.times(NS, j + 1 - NS))
                hi(b_gu[half, :, gu_cols(j)],
                   b_raw[half, 0:2 * F].rearrange("p (g f) -> p g f", g=2)[:, :, gu_cols(j)]
                   ).then_inc(b_hi_done, 1)

            def b_down(tile, first=False):
                half, _ = b_half(tile)
                act.wait_ge(b_ld[tile.parity], tile.of_parity(16 * SAMPLES))
                if not first:
                    act.wait_ge(d_mm, tile.times(1))
                hi(b_dn[half, :], b_raw[half, BD0:]).then_inc(bd_hi_done, 1)

            def mix(tile, first=False):
                act.wait_ge(mix_ld, tile.times(16 * SAMPLES, 16 * SAMPLES))
                if not first:
                    act.wait_ge(mix_mm, tile.times(1))
                hi(mix_hi[:], mix_raw[:]).then_inc(mix_hi_done, 1)

            def silu(tile, j, first=False):
                q = tile.times(NS, j)
                act.wait_ge(gate_mm, q + 1)
                if not first:
                    act.wait_ge(at_mm, tile.times(NS, -1 if j == 0 else 0))
                nc.scalar.activation(act_sb[:, gu_cols(j)], gu_out(j, 0), ACT.Silu).then_inc(silu_done, 1)

            def act_t(tile, b, first=False):
                s = (tile.parity * NS + b) % 2
                act.wait_ge(at_mm, tile.times(NS, b + 1))
                if not (first and b < 2):
                    act.wait_ge(dn_mm, tile.times(NS, b - 1))
                n = len(batches[b])
                full = n if chunk_rows[batches[b][-1]] == P else n - 1
                last = hi(at_hi[:, s, 0:full, :], tr_ps[:, 0:full * P].rearrange("p (c n) -> p c n", n=P))
                if full < n:
                    r = chunk_rows[-1]
                    last = hi(at_hi[0:r, s, full, :], tr_ps[0:r, full * P:n * P])
                last.then_inc(at_hi_done, 1)

            def t_t(tile):
                act.wait_ge(tt_mm, tile.times(1, 1))
                hi(tt_hi[:], tt_ps).then_inc(tt_hi_done, 1)

            def td_t(tile, first=False):
                act.wait_ge(tdt_mm, tile.times(1, 1))
                if not first:
                    act.wait_ge(d_mm, tile.times(1))
                hi(tdt_hi[:], tdt_ps).then_inc(tdt_hi_done, 1)

            def h_part(tile, first=False):
                act.wait_ge(h_done, tile.times(1, 1))
                if not first:
                    act.wait_ge(mix_mm, tile.times(1))
                hi(h_hi[:], xr[:, tile.parity, :]).then_inc(h_hi_done, 1)

            def step(i, prev=True, nxt=True, head=False, second=False):
                if nxt:
                    xt(i + 1, first=head)
                if prev:
                    mix(i - 1, first=second)
                    act_t(i - 1, 2)
                t_t(i)
                if nxt:
                    a_gu(i + 1)
                silu(i, 0, first=head)
                silu(i, 1, first=head)
                if head:
                    for n in range(8, GU_PIECES):
                        weights(n)
                if nxt:
                    b_slice(i + 1, 0)
                act_t(i, 0, first=head)
                if head:
                    for n in range(GU_PIECES, GU_PIECES + 2):
                        weights(n)
                a_down(i, first=head)
                if nxt:
                    b_slice(i + 1, 1)
                if prev:
                    td_t(i - 1, first=second)
                if head:
                    for n in range(GU_PIECES + 2, GU_PIECES + 4):
                        weights(n)
                silu(i, 2, first=head)
                act_t(i, 1, first=head)
                if head:
                    for n in range(GU_PIECES + 4, len(pieces)):
                        weights(n)
                if prev:
                    h_part(i - 1, first=second)
                if nxt:
                    b_slice(i + 1, 2)
                b_down(i, first=head)

            t0 = Tile(0, 0)
            xt(t0, first=True)
            a_gu(t0, first=True)
            for n in range(0, 6):
                weights(n)
            for j in range(NS):
                b_slice(t0, j, first=True)
            for n in range(6, 8):
                weights(n)
            step(t0, prev=False, head=True)
            step(t0 + 1, second=True)
            with act.Fori(1, (TILES - 2) // 2) as pair:
                step(Tile(pair, 0))
                step(Tile(pair, 1))
            step(Tile(0, TILES - 2))
            step(Tile(0, TILES - 1), nxt=False)
            last = Tile(0, TILES - 1)
            mix(last)
            act_t(last, 2)
            td_t(last)
            h_part(last)

        @block.vector
        def _(dve):
            def lo(dst, src, his):
                return nc.vector.tensor_tensor(dst, src, his.bitcast(F32), ALU.subtract)

            def weights(n):
                dve.wait_ge(w_hi_done, n + 1)
                lo(pieces[n][1], slot(n), pieces[n][0]).then_inc(w_done, 1)

            def xt(tile):
                dve.wait_ge(xt_hi_done, tile.times(1, 1))
                lo(xt_lo[:, tile.parity], xt_raw[:], xt_hi[:, tile.parity]).then_inc(xt_done, 1)

            def a_gu(tile):
                dve.wait_ge(agu_hi_done, tile.times(1, 1))
                lo(a_gu_to(wgu_lo), a_gu_from(tile), a_gu_to(wgu_hi)).then_inc(agu_done, 1)

            def a_down(tile):
                dve.wait_ge(ad_hi_done, tile.times(1, 1))
                lo(a_down_to(wd_lo), a_down_from(tile), a_down_to(wd_hi)).then_inc(ad_done, 1)

            def b_slice(tile, j):
                half, other = b_half(tile)
                dve.wait_ge(b_hi_done, tile.times(NS, j + 1))
                lo(b_gu[other, :, gu_cols(j)],
                   b_raw[half, 0:2 * F].rearrange("p (g f) -> p g f", g=2)[:, :, gu_cols(j)],
                   b_gu[half, :, gu_cols(j)]).then_inc(b_done, 1)

            def b_down(tile):
                half, other = b_half(tile)
                dve.wait_ge(bd_hi_done, tile.times(1, 1))
                lo(b_dn[other, :], b_raw[half, BD0:], b_dn[half, :]).then_inc(bd_done, 1)

            def mix(tile):
                dve.wait_ge(mix_hi_done, tile.times(1, 1))
                lo(mix_lo[:], mix_raw[:], mix_hi[:]).then_inc(mix_done, 1)

            def mul(tile, j):
                dve.wait_ge(silu_done, tile.times(NS, j + 1))
                dve.wait_ge(up_mm, tile.times(NS, j + 1))
                s = act_sb[:, gu_cols(j)]
                nc.vector.tensor_tensor(s, gu_out(j, 1), s, ALU.mult).then_inc(mul_done, 1)

            def act_t(tile, b):
                s = (tile.parity * NS + b) % 2
                dve.wait_ge(at_hi_done, tile.times(NS, b + 1))
                n = len(batches[b])
                full = n if chunk_rows[batches[b][-1]] == P else n - 1
                last = lo(at_lo[:, s, 0:full, :], tr_ps[:, 0:full * P].rearrange("p (c n) -> p c n", n=P),
                          at_hi[:, s, 0:full, :])
                if full < n:
                    r = chunk_rows[-1]
                    last = lo(at_lo[0:r, s, full, :], tr_ps[0:r, full * P:n * P], at_hi[0:r, s, full, :])
                last.then_inc(at_done, 1)

            def t_mask(tile, first=False):
                dve.wait_ge(t_mm, tile.times(1, 1))
                if not first:
                    dve.wait_ge(tt_mm, tile.times(1))
                for g in range(2):
                    for d in range(2):
                        last = nc.vector.tensor_tensor(t_own[:, g, d, :], gu_ps[g][:, 0:SR], own[:], ALU.mult)
                last.then_inc(t_done, 1)

            def td_mask(tile, first=False):
                dve.wait_ge(dn_mm, tile.times(NS, NS))
                if not first:
                    dve.wait_ge(tdt_mm, tile.times(1))
                for d in range(2):
                    last = nc.vector.tensor_tensor(td_own[:, d, :], td_ps, own[:], ALU.mult)
                last.then_inc(td_done, 1)

            def t_t(tile):
                dve.wait_ge(tt_hi_done, tile.times(1, 1))
                lo(tt_lo[:], tt_ps, tt_hi[:]).then_inc(tt_done, 1)

            def td_t(tile):
                dve.wait_ge(tdt_hi_done, tile.times(1, 1))
                lo(tdt_lo[:], tdt_ps, tdt_hi[:]).then_inc(tdt_done, 1)

            def h_sum(tile):
                dve.wait_ge(d_mm, tile.times(1, 1))
                dve.wait_ge(x_ld[tile.parity], tile.of_parity(16))
                rows = xr[:, tile.parity, :].rearrange("p (a n) -> p a n", a=2)
                nc.vector.tensor_tensor(rows, d_ps, rows, ALU.add).then_inc(h_done, 1)

            def h_part(tile):
                dve.wait_ge(h_hi_done, tile.times(1, 1))
                lo(h_lo[:], xr[:, tile.parity, :], h_hi[:]).then_inc(h_split, 1)

            def out_sum(tile):
                dve.wait_ge(mix_mm, tile.times(1, 1))
                nc.vector.tensor_tensor(xr[:, tile.parity, :], mix_ps, xr[:, tile.parity, :],
                                        ALU.add).then_inc(out_done, 1)

            def step(i, prev=True, nxt=True, head=False, second=False):
                if nxt:
                    xt(i + 1)
                if prev:
                    mix(i - 1)
                    act_t(i - 1, 2)
                t_mask(i, first=head)
                t_t(i)
                if nxt:
                    a_gu(i + 1)
                if prev:
                    td_mask(i - 1, first=second)
                mul(i, 0)
                if head:
                    for n in range(8, GU_PIECES):
                        weights(n)
                if nxt:
                    b_slice(i + 1, 0)
                mul(i, 1)
                act_t(i, 0)
                if head:
                    for n in range(GU_PIECES, GU_PIECES + 2):
                        weights(n)
                a_down(i)
                if nxt:
                    b_slice(i + 1, 1)
                if prev:
                    td_t(i - 1)
                if head:
                    for n in range(GU_PIECES + 2, GU_PIECES + 4):
                        weights(n)
                if prev:
                    h_sum(i - 1)
                act_t(i, 1)
                if head:
                    for n in range(GU_PIECES + 4, len(pieces)):
                        weights(n)
                if prev:
                    h_part(i - 1)
                mul(i, 2)
                if nxt:
                    b_slice(i + 1, 2)
                b_down(i)
                if prev:
                    out_sum(i - 1)

            nc.vector.memset(own[:], 0.0).then_inc(own_zero, 1)
            dve.wait_ge(own_zero, 1)
            for s in range(SAMPLES):
                nc.vector.memset(own[ROWS * s:ROWS * (s + 1), RANK * s:RANK * (s + 1)], LORA_SCALE
                                 ).then_inc(own_set, 1)
            dve.wait_ge(own_set, SAMPLES)
            t0 = Tile(0, 0)
            xt(t0)
            a_gu(t0)
            for n in range(0, 6):
                weights(n)
            for j in range(NS):
                b_slice(t0, j)
            for n in range(6, 8):
                weights(n)
            step(t0, prev=False, head=True)
            step(t0 + 1, second=True)
            with dve.Fori(1, (TILES - 2) // 2) as pair:
                step(Tile(pair, 0))
                step(Tile(pair, 1))
            step(Tile(0, TILES - 2))
            step(Tile(0, TILES - 1), nxt=False)
            last = Tile(0, TILES - 1)
            mix(last)
            act_t(last, 2)
            td_mask(last)
            td_t(last)
            h_sum(last)
            h_part(last)
            out_sum(last)

        @block.tensor
        def _(pe):
            def t_transpose(tile, first=False):
                pe.wait_ge(t_done, tile.times(1, 1))
                if not first:
                    pe.wait_ge(tt_done, tile.times(1))
                for g in range(2):
                    last = nc.tensor.transpose(tt_ps[:, g, :], t_own[:, g].rearrange("p d n -> p (d n)"),
                                               ident[:])
                last.then_inc(tt_mm, 1)

            def dense(tile, j, g, head=False):
                if j == 0 and g == 0:
                    pe.wait_ge(xt_done, tile.times(1, 1))
                    pe.wait_ge(agu_done, tile.times(1, 1))
                if g == 0:
                    if not (head and j < 2):
                        pe.wait_ge(mul_done, tile.times(NS, j - 1))
                elif not (head and j == 0):
                    pe.wait_ge(silu_done, tile.times(NS, j))
                ps = gu_ps[(2 * j + g) % 3][:, 0:SW]
                p = tile.parity
                for c in range(HC):
                    if head and c % 2 == 0:
                        pe.wait_ge(w_done, piece_of(g, j, c) + 1)
                    w_hi, w_lo = (w[:, g, c, SW * j:SW * (j + 1)] for w in (wgu_hi, wgu_lo))
                    nc.tensor.matmul(ps, xt_hi[:, p, c, :], w_hi, start=(c == 0), stop=False)
                    nc.tensor.matmul(ps, xt_hi[:, p, c, :], w_lo, start=False, stop=False)
                    last = nc.tensor.matmul(ps, xt_lo[:, p, c, :], w_hi, start=False,
                                            stop=(j == 0 and c == HC - 1))
                if j == 0 and g == 1:
                    last.then_inc(t_mm, 1)

            def adapt(tile, j, g):
                if g == 0:
                    if j == 0:
                        pe.wait_ge(tt_done, tile.times(1, 1))
                    pe.wait_ge(b_done, tile.times(NS, j + 1))
                ps = gu_out(j, g)
                nc.tensor.matmul(ps, tt_hi[:, g, :], b_gu[:, g, gu_cols(j)], start=False, stop=False,
                                 skip_group_check=(j == 0))
                nc.tensor.matmul(ps, tt_lo[:, g, :], b_gu[:, g, gu_cols(j)], start=False, stop=True,
                                 skip_group_check=(j == 0)).then_inc(up_mm if g else gate_mm, 1)

            def act_transpose(tile, b, head=False):
                pe.wait_ge(mul_done, tile.times(NS, b + 1))
                if not (head and b == 0):
                    pe.wait_ge(at_done, tile.times(NS, b))
                for n, k in enumerate(batches[b]):
                    r = chunk_rows[k]
                    last = nc.tensor.transpose(tr_ps[0:r, P * n:P * (n + 1)], act_sb[:, P * k:P * k + r],
                                               ident[:])
                last.then_inc(at_mm, 1)

            def down(tile, b, head=False):
                s = (tile.parity * NS + b) % 2
                pe.wait_ge(at_done, tile.times(NS, b + 1))
                if b == 0:
                    pe.wait_ge(ad_done, tile.times(1, 1))
                    if not head:
                        pe.wait_ge(h_done, tile.times(1))
                for n, k in enumerate(batches[b]):
                    if head:
                        pe.wait_ge(w_done, GU_PIECES + k // 2 + 1)
                    r = chunk_rows[k]
                    for t, (a, w) in enumerate(((at_hi, wd_hi), (at_hi, wd_lo), (at_lo, wd_hi))):
                        for half, cols in enumerate((slice(0, HH), slice(HH, H + SR))):
                            last = nc.tensor.matmul(d_banks[:, half, 0:cols.stop - cols.start], a[0:r, s, n, :],
                                                    w[0:r, k, cols], start=(k == 0 and t == 0),
                                                    stop=(k == FC - 1 and t == 2))
                last.then_inc(dn_mm, 1)

            def td_transpose(tile):
                pe.wait_ge(td_done, tile.times(1, 1))
                nc.tensor.transpose(tdt_ps, td_own[:].rearrange("p d n -> p (d n)"), ident[:]
                                    ).then_inc(tdt_mm, 1)

            def adapt_down(tile):
                pe.wait_ge(tdt_done, tile.times(1, 1))
                pe.wait_ge(bd_done, tile.times(1, 1))
                for half in range(2):
                    cols = b_dn[:, HH * half:HH * (half + 1)]
                    nc.tensor.matmul(d_ps[:, half], tdt_hi[:], cols, start=False, stop=False,
                                     skip_group_check=True)
                    last = nc.tensor.matmul(d_ps[:, half], tdt_lo[:], cols, start=False, stop=True,
                                            skip_group_check=True)
                last.then_inc(d_mm, 1)

            def mix(tile, second=False):
                pe.wait_ge(mix_done, tile.times(1, 1))
                pe.wait_ge(h_split, tile.times(1, 1))
                if not second:
                    pe.wait_ge(out_done, tile.times(1))
                nc.tensor.matmul(mix_ps, mix_hi[:], h_hi[:], start=True, stop=False)
                nc.tensor.matmul(mix_ps, mix_lo[:], h_hi[:], start=False, stop=False)
                nc.tensor.matmul(mix_ps, mix_hi[:], h_lo[:], start=False, stop=True).then_inc(mix_mm, 1)

            def step(i, prev=True, head=False, second=False):
                dense(i, 0, 0, head=head)
                dense(i, 0, 1, head=head)
                if prev:
                    act_transpose(i - 1, 2)
                dense(i, 1, 0, head=head)
                t_transpose(i, first=head)
                if prev:
                    down(i - 1, 2, head=second)
                adapt(i, 0, 0)
                adapt(i, 0, 1)
                adapt(i, 1, 0)
                dense(i, 1, 1, head=head)
                adapt(i, 1, 1)
                act_transpose(i, 0, head=head)
                dense(i, 2, 0, head=head)
                if prev:
                    td_transpose(i - 1)
                dense(i, 2, 1, head=head)
                if prev:
                    adapt_down(i - 1)
                adapt(i, 2, 0)
                adapt(i, 2, 1)
                act_transpose(i, 1, head=head)
                down(i, 0, head=head)
                if prev:
                    mix(i - 1, second=second)
                down(i, 1, head=head)

            t0 = Tile(0, 0)
            pe.wait_ge(consts, 1)
            step(t0, prev=False, head=True)
            step(t0 + 1, second=True)
            with pe.Fori(1, (TILES - 2) // 2) as pair:
                step(Tile(pair, 0))
                step(Tile(pair, 1))
            step(Tile(0, TILES - 2))
            step(Tile(0, TILES - 1))
            last = Tile(0, TILES - 1)
            act_transpose(last, 2)
            down(last, 2)
            td_transpose(last)
            adapt_down(last)
            mix(last)


def kernel(**inputs):
    import numpy as np
    import concourse.bacc as bacc
    from concourse.bass_utils import run_bass_kernel_spmd

    given = {k: np.asarray(v) for k, v in inputs.items()}
    x = given["x"]
    rows, hidden = x.shape[0] * x.shape[1], x.shape[2]
    tiles, hc = rows // P, hidden // P
    wg, wu, wd = (given[f"L0_cond_W_{n}"] for n in ("gate", "up", "down"))
    f = wg.shape[0]
    fc = -(-f // P)

    def by_partition(a):
        a = np.pad(a, ((0, 0), (0, 0), (0, -a.shape[2] % P)))
        return a.reshape(a.shape[0], a.shape[1], -1, P).transpose(0, 3, 2, 1)

    ag, au, ad = (given[f"L0_cond_A_{n}"][0] for n in ("gate", "up", "down"))
    bg, bu, bd = (given[f"L0_cond_B_{n}"][0] for n in ("gate", "up", "down"))
    n_adapters = ag.shape[0]
    a_gu = np.stack([by_partition(ag), by_partition(au)], axis=2)
    a_all = np.concatenate([a_gu.reshape(n_adapters, P, -1), by_partition(ad).reshape(n_adapters, P, -1)],
                           axis=2)
    b_all = np.concatenate([b.transpose(0, 2, 1) for b in (bg, bu, bd)], axis=2)
    arrays = {
        "x_rows": x.reshape(tiles, P, hidden),
        "x_cols": x.reshape(tiles, P, hc, P).transpose(0, 3, 2, 1),
        "w_gu": np.stack([w.T.reshape(hc, P, f) for w in (wg, wu)]),
        "w_down": np.pad(wd.T, ((0, fc * P - f), (0, 0))).reshape(fc, P, hidden),
        "a_all": a_all,
        "b_all": b_all,
        "w_mix": given["L1_cond_weights"],
        "idx_lora": given["itok_B_2_6"],
        "idx_mix": given["itok_B_0_15"],
    }
    arrays = {k: np.ascontiguousarray(v) for k, v in arrays.items()}
    nc = bacc.Bacc("TRN2", target_bir_lowering=False, num_devices=1, dynamic_dma_scratch_size=1024)
    args = [nc.dram_tensor(f"in_{k}", v.shape, mybir.dt.from_np(v.dtype), kind="ExternalInput").ap()
            for k, v in arrays.items()]
    out = nc.dram_tensor("out_0", (tiles, P, hidden), F32, kind="ExternalOutput").ap()
    build(nc, *args, out)
    r = run_bass_kernel_spmd(nc, [{f"in_{k}": v for k, v in arrays.items()}], core_ids=[0])
    return r.results[0]["out_0"].reshape(x.shape)
```

```python
from contextlib import ExitStack

import concourse.bass as bass
from concourse import mybir

F32 = mybir.dt.float32
F32R = mybir.dt.float32r
I32 = mybir.dt.int32
ACT = mybir.ActivationFunctionType
ALU = mybir.AluOpType

P = 128
LORA_SCALE = 0.5
WARM_UP = 56


class Tile:

    def __init__(self, pair, offset):
        self.pair, self.offset = pair, offset
        self.parity = offset % 2

    def __add__(self, n):
        return Tile(self.pair, self.offset + n)

    def __sub__(self, n):
        return Tile(self.pair, self.offset - n)

    def times(self, k, plus=0):
        return self.pair * (2 * k) + (k * self.offset + plus)

    def of_parity(self, k):
        return self.pair * k + k * (self.offset // 2 + 1)


def build(nc, x_rows, x_cols, w_gu, w_down, a_all, b_all, w_mix, indices, out):
    TILES, _, H = x_rows.shape
    HC = H // P
    F = w_gu.shape[3]
    SAMPLES = 4
    ROWS = P // SAMPLES
    RANK = b_all.shape[1]
    SR = SAMPLES * RANK
    NS = 3
    SW = (SR + F) // NS
    starts = [max(0, SW * j - SR) for j in range(NS)]
    widths = [SW * (j + 1) - SR - starts[j] for j in range(NS)]
    assert NS * SW == SR + F and SW % 2 == 0 and SW <= 512
    FC = -(-F // P)
    chunk_rows = [min(P, F - P * k) for k in range(FC)]
    batches = [range(0, starts[1] // P), range(starts[1] // P, starts[2] // P), range(starts[2] // P, FC)]
    BATCH = max(len(b) for b in batches)
    AGU = HC * 2 * RANK
    AD = FC * RANK
    BD0 = 2 * F
    BROW = 2 * F + H
    STAGE = H
    HH = H // 2
    assert 2 * SR == P and SW <= STAGE and HH + SR <= 512 and 2 * STAGE <= min(F, SAMPLES * (AGU + AD))

    with ExitStack() as ctx:
        def sb(name, shape, dt=F32):
            return ctx.enter_context(nc.sbuf_tensor(name, shape, dt))

        def bank(name):
            return ctx.enter_context(nc.psum_tensor(name, [P, 512], F32))

        def sem(name):
            return ctx.enter_context(nc.semaphore(name))

        wgu_hi = sb("wgu_hi", [P, 2, HC, SR + F], F32R)
        wgu_lo = sb("wgu_lo", [P, 2, HC, SR + F], F32R)
        wd_hi = sb("wd_hi", [P, FC, H + SR], F32R)
        wd_lo = sb("wd_lo", [P, FC, H + SR], F32R)
        stage = sb("stage", [P, 4, STAGE])
        a_raw = sb("a_raw", [P, 2, SAMPLES, AGU + AD])
        b_raw = sb("b_raw", [P, BROW])
        b_gu = sb("b_gu", [P, 2, F], F32R)
        b_dn = sb("b_dn", [P, H], F32R)
        mix_raw = sb("mix_raw", [P, P])
        mix_hi = sb("mix_hi", [P, P], F32R)
        mix_lo = sb("mix_lo", [P, P], F32R)
        xt_raw = sb("xt_raw", [P, HC, P])
        xt_hi = sb("xt_hi", [P, 2, HC, P], F32R)
        xt_lo = sb("xt_lo", [P, 2, HC, P], F32R)
        xr = sb("xr", [P, 2, H])
        h_hi = sb("h_hi", [P, H], F32R)
        h_lo = sb("h_lo", [P, H], F32R)
        act_sb = sb("act_sb", [P, F])
        at_hi = sb("at_hi", [P, 2, BATCH, P], F32R)
        at_lo = sb("at_lo", [P, 2, BATCH, P], F32R)
        t_own = sb("t_own", [P, 2, 2, SR])
        tt_hi = sb("tt_hi", [P, 2, P], F32R)
        tt_lo = sb("tt_lo", [P, 2, P], F32R)
        td_own = sb("td_own", [P, 2, SR])
        tdt_hi = sb("tdt_hi", [P, P], F32R)
        tdt_lo = sb("tdt_lo", [P, P], F32R)
        own = sb("own", [P, SR])
        ident = sb("ident", [P, P])
        idx = sb("idx", [1, 2, indices.shape[2]], I32)

        gu_ps = [bank(f"gu_ps{n}") for n in range(3)]
        d_banks = ctx.enter_context(nc.psum_tensor("d_banks", [P, 2, 512], F32))
        d_ps = d_banks[:, :, 0:HH]
        td_ps = d_banks[:, 1, HH:HH + SR]
        mix_ps = bank("mix_ps")[:, 0:H]
        tr_ps = bank("tr_ps")
        t_bank = bank("t_bank")
        tt_ps = t_bank[:, 0:2 * P].rearrange("p (g n) -> p g n", g=2)
        tdt_ps = t_bank[:, 2 * P:3 * P]

        idx_ld = sem("idx_ld")
        w_ld = [sem(f"w_ld{n}") for n in range(10)]
        xt_ld = sem("xt_ld")
        a_ld = [sem(f"a_ld{n}") for n in range(2)]
        b_ld = [sem(f"b_ld{n}") for n in range(2)]
        mix_ld = sem("mix_ld")
        x_ld = [sem(f"x_ld{n}") for n in range(2)]
        stored = [sem(f"stored{n}") for n in range(2)]
        zeroed = sem("zeroed")
        consts = sem("consts")
        own_zero = sem("own_zero")
        own_set = sem("own_set")
        mix_zero = sem("mix_zero")
        w_hi_done = sem("w_hi_done")
        w_done = sem("w_done")
        xt_hi_done = sem("xt_hi_done")
        xt_done = sem("xt_done")
        agu_hi_done = sem("agu_hi_done")
        agu_done = sem("agu_done")
        ad_hi_done = sem("ad_hi_done")
        ad_done = sem("ad_done")
        b_hi_done = sem("b_hi_done")
        b_done = sem("b_done")
        bd_hi_done = sem("bd_hi_done")
        bd_done = sem("bd_done")
        mix_hi_done = sem("mix_hi_done")
        mix_done = sem("mix_done")
        gate_mm = sem("gate_mm")
        up_mm = sem("up_mm")
        silu_done = sem("silu_done")
        mul_done = sem("mul_done")
        at_mm = sem("at_mm")
        at_hi_done = sem("at_hi_done")
        at_done = sem("at_done")
        dn_mm = sem("dn_mm")
        t_mm = sem("t_mm")
        t_done = sem("t_done")
        tt_mm = sem("tt_mm")
        tt_hi_done = sem("tt_hi_done")
        tt_done = sem("tt_done")
        td_done = sem("td_done")
        tdt_mm = sem("tdt_mm")
        tdt_hi_done = sem("tdt_hi_done")
        tdt_done = sem("tdt_done")
        d_mm = sem("d_mm")
        h_done = sem("h_done")
        h_hi_done = sem("h_hi_done")
        h_split = sem("h_split")
        mix_mm = sem("mix_mm")
        out_done = sem("out_done")

        pieces = []
        for j in range(NS):
            for g in range(2):
                for c in range(HC):
                    fs = slice(starts[j], starts[j] + widths[j])
                    ws = slice(SR + starts[j], SR + starts[j] + widths[j])
                    pieces.append((wgu_hi[:, g, c, ws], wgu_lo[:, g, c, ws], w_gu[g, c, :, fs]))
        GU_PIECES = len(pieces)
        for k, n in enumerate(chunk_rows):
            pieces.append((wd_hi[0:n, k, 0:H], wd_lo[0:n, k, 0:H], w_down[k, 0:n, :]))

        slots = [stage[:, n, :] for n in range(4)]
        slots += [xr[:, n, :] for n in range(2)]
        a_flat = a_raw[:, 1].rearrange("p s n -> p (s n)")
        slots += [buf[:, STAGE * n:STAGE * (n + 1)] for buf in (a_flat, act_sb) for n in range(2)]
        slot_no = [*range(10), *range(8)]
        A_PIECES, ACT_PIECES = 18, 10
        slot_no += [n % 6 for n in range(len(pieces) - len(slot_no))]

        def slot(n):
            to = pieces[n][0]
            return slots[slot_no[n]][0:to.shape[0], 0:to.shape[1]]

        def before_in_slot(n):
            return [m for m in range(n) if slot_no[m] == slot_no[n]]

        def piece_of(g, j, c):
            return (j * 2 + g) * HC + c

        def b_half(tile):
            return (slice(0, SR), slice(SR, P)) if tile.parity == 0 else (slice(SR, P), slice(0, SR))

        def gu_cols(j):
            return slice(starts[j], starts[j] + widths[j])

        def gu_out(j, g):
            return gu_ps[(2 * j + g) % 3][:, SW - widths[j]:SW]

        def a_gu_to(w):
            return w[:, :, :, 0:SR].rearrange("p g c (s r) -> p s (g c) r", s=SAMPLES)

        def a_gu_from(tile):
            return a_raw[:, tile.parity, :, 0:AGU].rearrange("p s (n r) -> p s n r", r=RANK)

        def a_down_to(w):
            return w[:, :, H:].rearrange("p k (s r) -> p s k r", s=SAMPLES)

        def a_down_from(tile):
            return a_raw[:, tile.parity, :, AGU:].rearrange("p s (k r) -> p s k r", r=RANK)

        block = ctx.enter_context(nc.Block())

        @block.sync
        def _(sp):
            def load_xt(tile, first=False):
                at = sp.snap(tile.times(1))
                if not first:
                    sp.wait_ge(xt_done, tile.times(1))
                sp.dma_start(xt_raw[:], x_cols[bass.ds(at, 1)].rearrange("a p c n -> p (a c) n")
                             ).then_inc(xt_ld, 16)

            def adapters(tile):
                return [sp.value_load(idx[0:1, 0, bass.ds(tile.times(SAMPLES, s), 1)], min_val=0,
                                      max_val=a_all.shape[0] - 1) for s in range(SAMPLES)]

            def load_a(tile, which, first=False):
                if not first:
                    sp.wait_ge(ad_done, tile.times(1, -1))
                for s in range(SAMPLES):
                    sp.dma_start(a_raw[:, tile.parity, s, :],
                                 a_all[bass.ds(which[s], 1)].rearrange("a p n -> (a p) n")
                                 ).then_inc(a_ld[tile.parity], 16)

            def load_b(tile, which, first=False):
                if not first:
                    sp.wait_ge(bd_done, tile.times(1, -1))
                for s in range(SAMPLES):
                    at = SR * tile.parity + RANK * s
                    sp.dma_start(b_raw[at:at + RANK, :],
                                 b_all[bass.ds(which[s], 1)].rearrange("a r n -> (a r) n")
                                 ).then_inc(b_ld[tile.parity], 16)

            def load_mix(tile, first=False):
                which = [sp.value_load(idx[0:1, 1, bass.ds(tile.times(SAMPLES, s), 1)], min_val=0,
                                       max_val=w_mix.shape[0] - 1) for s in range(SAMPLES)]
                if not first:
                    sp.wait_ge(mix_done, tile.times(1))
                for s in range(SAMPLES):
                    rs = slice(ROWS * s, ROWS * (s + 1))
                    sp.dma_start(mix_raw[rs, rs], w_mix[bass.ds(which[s], 1)].rearrange("a c d -> (a c) d")
                                 ).then_inc(mix_ld, 16)

            def load_x(tile, first=False):
                at = sp.snap(tile.times(1))
                if not first:
                    sp.wait_ge(stored[tile.parity], (tile - 2).of_parity(16))
                sp.dma_start(xr[:, tile.parity, :], x_rows[bass.ds(at, 1)].rearrange("a p h -> (a p) h")
                             ).then_inc(x_ld[tile.parity], 16)

            def store(tile):
                at = sp.snap(tile.times(1))
                sp.wait_ge(out_done, tile.times(1, 1))
                sp.dma_start(out[bass.ds(at, 1)].rearrange("a p h -> (a p) h"), xr[:, tile.parity, :]
                             ).then_inc(stored[tile.parity], 16)

            def load_piece(n):
                if before_in_slot(n):
                    sp.wait_ge(w_done, before_in_slot(n)[-1] + 1)
                sp.dma_start(slot(n), pieces[n][2]).then_inc(w_ld[slot_no[n]], 16)

            t0 = Tile(0, 0)
            sp.dma_start(idx[:], indices).then_inc(idx_ld, 16)
            load_xt(t0, first=True)
            for n in range(0, 2):
                load_piece(n)
            sp.wait_ge(idx_ld, 16)
            of_t0 = adapters(t0)
            load_a(t0, of_t0, first=True)
            for n in range(2, 12):
                load_piece(n)
            load_b(t0, of_t0, first=True)
            of_t1 = adapters(t0 + 1)
            for n in range(12, GU_PIECES):
                load_piece(n)
            load_xt(t0 + 1)
            for n in range(GU_PIECES, GU_PIECES + 4):
                load_piece(n)
            sp.wait_ge(w_done, A_PIECES)
            load_a(t0 + 1, of_t1, first=True)
            for n in range(GU_PIECES + 4, GU_PIECES + 8):
                load_piece(n)
            load_b(t0 + 1, of_t1, first=True)
            for n in range(GU_PIECES + 8, len(pieces)):
                load_piece(n)
            load_xt(t0 + 2)
            sp.wait_ge(mix_zero, 1)
            load_mix(t0, first=True)
            of_t2 = adapters(t0 + 2)
            sp.wait_ge(w_done, len(pieces))
            load_x(t0, first=True)
            load_a(t0 + 2, of_t2)
            load_b(t0 + 2, of_t2)

            def step(i, more=True, head=False):
                if more:
                    load_xt(i + 2)
                load_mix(i)
                if more:
                    which = adapters(i + 2)
                    load_a(i + 2, which)
                load_x(i, first=head)
                if more:
                    load_b(i + 2, which)
                store(i - 1)

            step(t0 + 1, head=True)
            with sp.Fori(1, (TILES - 2) // 2) as pair:
                step(Tile(pair, 0))
                step(Tile(pair, 1))
            step(Tile(0, TILES - 2), more=False)
            step(Tile(0, TILES - 1), more=False)
            last = Tile(0, TILES - 1)
            store(last)
            for tile in (last - 1, last):
                sp.wait_ge(stored[tile.parity], tile.of_parity(16))

        @block.gpsimd
        def _(pool):
            nc.gpsimd.memset(ident[:], 0.0).then_inc(zeroed, 1)
            pool.wait_ge(zeroed, 1)
            nc.gpsimd.affine_select(out=ident[:], in_=ident[:], compare_op=ALU.not_equal, fill=1.0, base=0,
                                    pattern=[[-1, P]], channel_multiplier=1).then_inc(consts, 1)
            nc.gpsimd.memset(mix_raw[:], 0.0).then_inc(mix_zero, 1)

        @block.scalar
        def _(act):
            def hi(dst, src):
                return nc.scalar.activation(dst, src, ACT.Copy)

            def weights(n):
                act.wait_ge(w_ld[slot_no[n]], 16 * (len(before_in_slot(n)) + 1))
                hi(pieces[n][0], slot(n)).then_inc(w_hi_done, 1)

            def xt(tile, first=False):
                act.wait_ge(xt_ld, tile.times(16, 16))
                if not first:
                    act.wait_ge(up_mm, tile.times(NS, -NS))
                hi(xt_hi[:, tile.parity], xt_raw[:]).then_inc(xt_hi_done, 1)

            def a_gu(tile, first=False):
                act.wait_ge(a_ld[tile.parity], tile.of_parity(16 * SAMPLES))
                if not first:
                    act.wait_ge(t_mm, tile.times(1))
                hi(a_gu_to(wgu_hi), a_gu_from(tile)).then_inc(agu_hi_done, 1)

            def a_down(tile, first=False):
                act.wait_ge(a_ld[tile.parity], tile.of_parity(16 * SAMPLES))
                if not first:
                    act.wait_ge(dn_mm, tile.times(NS))
                hi(a_down_to(wd_hi), a_down_from(tile)).then_inc(ad_hi_done, 1)

            def b_slice(tile, j, first=False):
                half, _ = b_half(tile)
                act.wait_ge(b_ld[tile.parity], tile.of_parity(16 * SAMPLES))
                if not first:
                    act.wait_ge(up_mm, tile.times(NS, j + 1 - NS))
                hi(b_gu[half, :, gu_cols(j)],
                   b_raw[half, 0:2 * F].rearrange("p (g f) -> p g f", g=2)[:, :, gu_cols(j)]
                   ).then_inc(b_hi_done, 1)

            def b_down(tile, first=False):
                half, _ = b_half(tile)
                act.wait_ge(b_ld[tile.parity], tile.of_parity(16 * SAMPLES))
                if not first:
                    act.wait_ge(d_mm, tile.times(1))
                hi(b_dn[half, :], b_raw[half, BD0:]).then_inc(bd_hi_done, 1)

            def mix(tile, first=False):
                act.wait_ge(mix_ld, tile.times(16 * SAMPLES, 16 * SAMPLES))
                if not first:
                    act.wait_ge(mix_mm, tile.times(1))
                hi(mix_hi[:], mix_raw[:]).then_inc(mix_hi_done, 1)

            def silu(tile, j, first=False):
                q = tile.times(NS, j)
                act.wait_ge(gate_mm, q + 1)
                if first:
                    act.wait_ge(w_done, ACT_PIECES)
                else:
                    act.wait_ge(at_mm, tile.times(NS, -1 if j == 0 else 0))
                nc.scalar.activation(act_sb[:, gu_cols(j)], gu_out(j, 0), ACT.Silu).then_inc(silu_done, 1)

            def act_t(tile, b, first=False):
                s = (tile.parity * NS + b) % 2
                act.wait_ge(at_mm, tile.times(NS, b + 1))
                if not (first and b < 2):
                    act.wait_ge(dn_mm, tile.times(NS, b - 1))
                n = len(batches[b])
                full = n if chunk_rows[batches[b][-1]] == P else n - 1
                last = hi(at_hi[:, s, 0:full, :], tr_ps[:, 0:full * P].rearrange("p (c n) -> p c n", n=P))
                if full < n:
                    r = chunk_rows[-1]
                    last = hi(at_hi[0:r, s, full, :], tr_ps[0:r, full * P:n * P])
                last.then_inc(at_hi_done, 1)

            def t_t(tile):
                act.wait_ge(tt_mm, tile.times(1, 1))
                hi(tt_hi[:], tt_ps).then_inc(tt_hi_done, 1)

            def td_t(tile, first=False):
                act.wait_ge(tdt_mm, tile.times(1, 1))
                if not first:
                    act.wait_ge(d_mm, tile.times(1))
                hi(tdt_hi[:], tdt_ps).then_inc(tdt_hi_done, 1)

            def h_part(tile, first=False):
                act.wait_ge(h_done, tile.times(1, 1))
                if not first:
                    act.wait_ge(mix_mm, tile.times(1))
                hi(h_hi[:], xr[:, tile.parity, :]).then_inc(h_hi_done, 1)

            def first_step(i):
                xt(i, first=True)
                for n in range(0, 2):
                    weights(n)
                a_gu(i, first=True)
                for n in range(2, 12):
                    weights(n)
                b_slice(i, 0, first=True)
                t_t(i)
                for n in range(12, 14):
                    weights(n)
                b_slice(i, 1, first=True)
                for n in range(14, 16):
                    weights(n)
                silu(i, 0, first=True)
                for n in range(16, 18):
                    weights(n)
                silu(i, 1, first=True)
                for n in range(18, 22):
                    weights(n)
                act_t(i, 0, first=True)
                a_down(i, first=True)
                for n in range(22, GU_PIECES):
                    weights(n)
                b_slice(i, 2, first=True)
                for n in range(GU_PIECES, GU_PIECES + 4):
                    weights(n)
                silu(i, 2, first=True)
                act_t(i, 1, first=True)
                xt(i + 1, first=True)
                a_gu(i + 1)
                for n in range(GU_PIECES + 4, len(pieces)):
                    weights(n)
                for j in range(NS):
                    b_slice(i + 1, j)
                b_down(i, first=True)

            def step(i, nxt=True, second=False):
                if nxt:
                    xt(i + 1)
                mix(i - 1, first=second)
                act_t(i - 1, 2)
                t_t(i)
                if nxt:
                    a_gu(i + 1)
                silu(i, 0)
                silu(i, 1)
                if nxt:
                    b_slice(i + 1, 0)
                act_t(i, 0)
                a_down(i)
                if nxt:
                    b_slice(i + 1, 1)
                td_t(i - 1, first=second)
                silu(i, 2)
                h_part(i - 1, first=second)
                act_t(i, 1)
                if nxt:
                    b_slice(i + 1, 2)
                b_down(i)

            act.wait_ge(consts, 1)
            nc.scalar.activation(t_own[0:1, 0, 0, 0:1], ident[0:1, 0:1], ACT.Silu)
            t0 = Tile(0, 0)
            first_step(t0)
            step(t0 + 1, second=True)
            with act.Fori(1, (TILES - 2) // 2) as pair:
                step(Tile(pair, 0))
                step(Tile(pair, 1))
            step(Tile(0, TILES - 2))
            step(Tile(0, TILES - 1), nxt=False)
            last = Tile(0, TILES - 1)
            act_t(last, 2)
            td_t(last)

        @block.vector
        def _(dve):
            def lo(dst, src, his):
                return nc.vector.tensor_tensor(dst, src, his.bitcast(F32), ALU.subtract)

            def weights(n):
                dve.wait_ge(w_hi_done, n + 1)
                lo(pieces[n][1], slot(n), pieces[n][0]).then_inc(w_done, 1)

            def xt(tile):
                dve.wait_ge(xt_hi_done, tile.times(1, 1))
                lo(xt_lo[:, tile.parity], xt_raw[:], xt_hi[:, tile.parity]).then_inc(xt_done, 1)

            def a_gu(tile):
                dve.wait_ge(agu_hi_done, tile.times(1, 1))
                lo(a_gu_to(wgu_lo), a_gu_from(tile), a_gu_to(wgu_hi)).then_inc(agu_done, 1)

            def a_down(tile):
                dve.wait_ge(ad_hi_done, tile.times(1, 1))
                lo(a_down_to(wd_lo), a_down_from(tile), a_down_to(wd_hi)).then_inc(ad_done, 1)

            def b_slice(tile, j):
                half, other = b_half(tile)
                dve.wait_ge(b_hi_done, tile.times(NS, j + 1))
                lo(b_gu[other, :, gu_cols(j)],
                   b_raw[half, 0:2 * F].rearrange("p (g f) -> p g f", g=2)[:, :, gu_cols(j)],
                   b_gu[half, :, gu_cols(j)]).then_inc(b_done, 1)

            def b_down(tile):
                half, other = b_half(tile)
                dve.wait_ge(bd_hi_done, tile.times(1, 1))
                lo(b_dn[other, :], b_raw[half, BD0:], b_dn[half, :]).then_inc(bd_done, 1)

            def mix(tile):
                dve.wait_ge(mix_hi_done, tile.times(1, 1))
                lo(mix_lo[:], mix_raw[:], mix_hi[:]).then_inc(mix_done, 1)

            def mul(tile, j):
                dve.wait_ge(silu_done, tile.times(NS, j + 1))
                dve.wait_ge(up_mm, tile.times(NS, j + 1))
                s = act_sb[:, gu_cols(j)]
                nc.vector.tensor_tensor(s, gu_out(j, 1), s, ALU.mult).then_inc(mul_done, 1)

            def act_t(tile, b):
                s = (tile.parity * NS + b) % 2
                dve.wait_ge(at_hi_done, tile.times(NS, b + 1))
                n = len(batches[b])
                full = n if chunk_rows[batches[b][-1]] == P else n - 1
                last = lo(at_lo[:, s, 0:full, :], tr_ps[:, 0:full * P].rearrange("p (c n) -> p c n", n=P),
                          at_hi[:, s, 0:full, :])
                if full < n:
                    r = chunk_rows[-1]
                    last = lo(at_lo[0:r, s, full, :], tr_ps[0:r, full * P:n * P], at_hi[0:r, s, full, :])
                last.then_inc(at_done, 1)

            def t_mask(tile, first=False):
                dve.wait_ge(t_mm, tile.times(1, 1))
                if not first:
                    dve.wait_ge(tt_mm, tile.times(1))
                for g in range(2):
                    for d in range(2):
                        last = nc.vector.tensor_tensor(t_own[:, g, d, :], gu_ps[g][:, 0:SR], own[:], ALU.mult)
                last.then_inc(t_done, 1)

            def td_mask(tile, first=False):
                dve.wait_ge(dn_mm, tile.times(NS, NS))
                if not first:
                    dve.wait_ge(tdt_mm, tile.times(1))
                for d in range(2):
                    last = nc.vector.tensor_tensor(td_own[:, d, :], td_ps, own[:], ALU.mult)
                last.then_inc(td_done, 1)

            def t_t(tile):
                dve.wait_ge(tt_hi_done, tile.times(1, 1))
                lo(tt_lo[:], tt_ps, tt_hi[:]).then_inc(tt_done, 1)

            def td_t(tile):
                dve.wait_ge(tdt_hi_done, tile.times(1, 1))
                lo(tdt_lo[:], tdt_ps, tdt_hi[:]).then_inc(tdt_done, 1)

            def h_sum(tile):
                dve.wait_ge(d_mm, tile.times(1, 1))
                dve.wait_ge(x_ld[tile.parity], tile.of_parity(16))
                rows = xr[:, tile.parity, :].rearrange("p (a n) -> p a n", a=2)
                nc.vector.tensor_tensor(rows, d_ps, rows, ALU.add).then_inc(h_done, 1)

            def h_part(tile):
                dve.wait_ge(h_hi_done, tile.times(1, 1))
                lo(h_lo[:], xr[:, tile.parity, :], h_hi[:]).then_inc(h_split, 1)

            def out_sum(tile):
                dve.wait_ge(mix_mm, tile.times(1, 1))
                nc.vector.tensor_tensor(xr[:, tile.parity, :], mix_ps, xr[:, tile.parity, :],
                                        ALU.add).then_inc(out_done, 1)

            def first_step(i):
                xt(i)
                for n in range(0, 2):
                    weights(n)
                a_gu(i)
                for n in range(2, 12):
                    weights(n)
                t_mask(i, first=True)
                b_slice(i, 0)
                t_t(i)
                for n in range(12, 14):
                    weights(n)
                b_slice(i, 1)
                for n in range(14, 16):
                    weights(n)
                mul(i, 0)
                for n in range(16, 22):
                    weights(n)
                mul(i, 1)
                act_t(i, 0)
                a_down(i)
                for n in range(22, GU_PIECES):
                    weights(n)
                b_slice(i, 2)
                for n in range(GU_PIECES, GU_PIECES + 4):
                    weights(n)
                act_t(i, 1)
                mul(i, 2)
                xt(i + 1)
                a_gu(i + 1)
                for n in range(GU_PIECES + 4, len(pieces)):
                    weights(n)
                for j in range(NS):
                    b_slice(i + 1, j)
                b_down(i)

            def step(i, nxt=True, second=False):
                if nxt:
                    xt(i + 1)
                mix(i - 1)
                act_t(i - 1, 2)
                t_mask(i)
                t_t(i)
                if nxt:
                    a_gu(i + 1)
                td_mask(i - 1, first=second)
                mul(i, 0)
                if nxt:
                    b_slice(i + 1, 0)
                mul(i, 1)
                act_t(i, 0)
                a_down(i)
                if nxt:
                    b_slice(i + 1, 1)
                td_t(i - 1)
                h_sum(i - 1)
                h_part(i - 1)
                act_t(i, 1)
                mul(i, 2)
                if nxt:
                    b_slice(i + 1, 2)
                b_down(i)
                out_sum(i - 1)

            nc.vector.memset(own[:], 0.0).then_inc(own_zero, 1)
            dve.wait_ge(own_zero, 1)
            for s in range(SAMPLES):
                nc.vector.memset(own[ROWS * s:ROWS * (s + 1), RANK * s:RANK * (s + 1)], LORA_SCALE
                                 ).then_inc(own_set, 1)
            dve.wait_ge(own_set, SAMPLES)
            t0 = Tile(0, 0)
            first_step(t0)
            step(t0 + 1, second=True)
            with dve.Fori(1, (TILES - 2) // 2) as pair:
                step(Tile(pair, 0))
                step(Tile(pair, 1))
            step(Tile(0, TILES - 2))
            step(Tile(0, TILES - 1), nxt=False)
            last = Tile(0, TILES - 1)
            act_t(last, 2)
            td_mask(last)
            td_t(last)
            h_sum(last)
            out_sum(last)

        @block.tensor
        def _(pe):
            def t_transpose(tile, first=False):
                pe.wait_ge(t_done, tile.times(1, 1))
                if not first:
                    pe.wait_ge(tt_done, tile.times(1))
                for g in range(2):
                    last = nc.tensor.transpose(tt_ps[:, g, :], t_own[:, g].rearrange("p d n -> p (d n)"),
                                               ident[:])
                last.then_inc(tt_mm, 1)

            def dense(tile, j, g, head=False):
                if j == 0 and g == 0:
                    pe.wait_ge(xt_done, tile.times(1, 1))
                    pe.wait_ge(agu_done, tile.times(1, 1))
                if g == 0:
                    if not (head and j < 2):
                        pe.wait_ge(mul_done, tile.times(NS, j - 1))
                elif not (head and j == 0):
                    pe.wait_ge(silu_done, tile.times(NS, j))
                ps = gu_ps[(2 * j + g) % 3][:, 0:SW]
                p = tile.parity
                for c in range(HC):
                    if head:
                        pe.wait_ge(w_done, piece_of(g, j, c) + 1)
                    w_hi, w_lo = (w[:, g, c, SW * j:SW * (j + 1)] for w in (wgu_hi, wgu_lo))
                    nc.tensor.matmul(ps, xt_hi[:, p, c, :], w_hi, start=(c == 0), stop=False)
                    nc.tensor.matmul(ps, xt_hi[:, p, c, :], w_lo, start=False, stop=False)
                    last = nc.tensor.matmul(ps, xt_lo[:, p, c, :], w_hi, start=False,
                                            stop=(j == 0 and c == HC - 1))
                if j == 0 and g == 1:
                    last.then_inc(t_mm, 1)

            def adapt(tile, j, g):
                if g == 0:
                    if j == 0:
                        pe.wait_ge(tt_done, tile.times(1, 1))
                    pe.wait_ge(b_done, tile.times(NS, j + 1))
                ps = gu_out(j, g)
                nc.tensor.matmul(ps, tt_hi[:, g, :], b_gu[:, g, gu_cols(j)], start=False, stop=False,
                                 skip_group_check=(j == 0))
                nc.tensor.matmul(ps, tt_lo[:, g, :], b_gu[:, g, gu_cols(j)], start=False, stop=True,
                                 skip_group_check=(j == 0)).then_inc(up_mm if g else gate_mm, 1)

            def act_transpose(tile, b, head=False):
                pe.wait_ge(mul_done, tile.times(NS, b + 1))
                if not (head and b == 0):
                    pe.wait_ge(at_done, tile.times(NS, b))
                for n, k in enumerate(batches[b]):
                    r = chunk_rows[k]
                    last = nc.tensor.transpose(tr_ps[0:r, P * n:P * (n + 1)], act_sb[:, P * k:P * k + r],
                                               ident[:])
                last.then_inc(at_mm, 1)

            def down(tile, b, head=False, part=slice(None), td_first=False):
                s = (tile.parity * NS + b) % 2
                pe.wait_ge(at_done, tile.times(NS, b + 1))
                if b == 0:
                    pe.wait_ge(ad_done, tile.times(1, 1))
                    if not head:
                        pe.wait_ge(h_done, tile.times(1))
                halves = (slice(0, HH), slice(HH, H + SR))
                for some in (((1,), (0,)) if td_first else ((0, 1),)):
                    for n, k in list(enumerate(batches[b]))[part]:
                        if head:
                            pe.wait_ge(w_done, GU_PIECES + k + 1)
                        r = chunk_rows[k]
                        for t, (a, w) in enumerate(((at_hi, wd_hi), (at_hi, wd_lo), (at_lo, wd_hi))):
                            for half in some:
                                cols = halves[half]
                                last = nc.tensor.matmul(d_banks[:, half, 0:cols.stop - cols.start],
                                                        a[0:r, s, n, :], w[0:r, k, cols],
                                                        start=(k == 0 and t == 0),
                                                        stop=(k == FC - 1 and t == 2))
                    if k == batches[b][-1] and some[-1] == 1:
                        last.then_inc(dn_mm, 1)

            def td_transpose(tile):
                pe.wait_ge(td_done, tile.times(1, 1))
                nc.tensor.transpose(tdt_ps, td_own[:].rearrange("p d n -> p (d n)"), ident[:]
                                    ).then_inc(tdt_mm, 1)

            def adapt_down(tile):
                pe.wait_ge(tdt_done, tile.times(1, 1))
                pe.wait_ge(bd_done, tile.times(1, 1))
                for half in range(2):
                    cols = b_dn[:, HH * half:HH * (half + 1)]
                    nc.tensor.matmul(d_ps[:, half], tdt_hi[:], cols, start=False, stop=False,
                                     skip_group_check=True)
                    last = nc.tensor.matmul(d_ps[:, half], tdt_lo[:], cols, start=False, stop=True,
                                            skip_group_check=True)
                last.then_inc(d_mm, 1)

            def mix(tile, second=False):
                pe.wait_ge(mix_done, tile.times(1, 1))
                pe.wait_ge(h_split, tile.times(1, 1))
                if not second:
                    pe.wait_ge(out_done, tile.times(1))
                nc.tensor.matmul(mix_ps, mix_hi[:], h_hi[:], start=True, stop=False)
                nc.tensor.matmul(mix_ps, mix_lo[:], h_hi[:], start=False, stop=False)
                nc.tensor.matmul(mix_ps, mix_hi[:], h_lo[:], start=False, stop=True).then_inc(mix_mm, 1)

            def last_mix(tile):
                pe.wait_ge(mix_ld, tile.times(16 * SAMPLES, 16 * SAMPLES))
                pe.wait_ge(h_done, tile.times(1, 1))
                pe.wait_ge(out_done, tile.times(1))
                nc.tensor.matmul(mix_ps, mix_raw[:], xr[:, tile.parity, :], start=True, stop=True
                                 ).then_inc(mix_mm, 1)

            def step(i, prev=True, head=False, second=False, tail=False):
                dense(i, 0, 0, head=head)
                dense(i, 0, 1, head=head)
                if prev:
                    act_transpose(i - 1, 2)
                dense(i, 1, 0, head=head)
                t_transpose(i, first=head)
                if prev:
                    down(i - 1, 2, head=second, part=slice(0, 3))
                adapt(i, 0, 0)
                if prev:
                    down(i - 1, 2, head=second, part=slice(3, None))
                adapt(i, 0, 1)
                adapt(i, 1, 0)
                dense(i, 1, 1, head=head)
                adapt(i, 1, 1)
                act_transpose(i, 0, head=head)
                dense(i, 2, 0, head=head)
                if prev:
                    td_transpose(i - 1)
                dense(i, 2, 1, head=head)
                if prev:
                    adapt_down(i - 1)
                adapt(i, 2, 0)
                adapt(i, 2, 1)
                act_transpose(i, 1, head=head)
                down(i, 0, head=head)
                if prev:
                    mix(i - 1, second=second)
                if tail:
                    act_transpose(i, 2)
                down(i, 1, head=head)

            pe.wait_ge(consts, 1)
            for _ in range(WARM_UP):
                nc.tensor.transpose(tr_ps[:, 0:P], ident[:], ident[:])
            t0 = Tile(0, 0)
            step(t0, prev=False, head=True)
            step(t0 + 1, second=True)
            with pe.Fori(1, (TILES - 2) // 2) as pair:
                step(Tile(pair, 0))
                step(Tile(pair, 1))
            step(Tile(0, TILES - 2))
            last = Tile(0, TILES - 1)
            step(last, tail=True)
            down(last, 2, td_first=True)
            td_transpose(last)
            adapt_down(last)
            last_mix(last)


def kernel(**inputs):
    import numpy as np
    import concourse.bacc as bacc
    from concourse.bass_utils import run_bass_kernel_spmd

    given = {k: np.asarray(v) for k, v in inputs.items()}
    x = given["x"]
    rows, hidden = x.shape[0] * x.shape[1], x.shape[2]
    tiles, hc = rows // P, hidden // P
    wg, wu, wd = (given[f"L0_cond_W_{n}"] for n in ("gate", "up", "down"))
    f = wg.shape[0]
    fc = -(-f // P)

    def by_partition(a):
        a = np.pad(a, ((0, 0), (0, 0), (0, -a.shape[2] % P)))
        return a.reshape(a.shape[0], a.shape[1], -1, P).transpose(0, 3, 2, 1)

    ag, au, ad = (given[f"L0_cond_A_{n}"][0] for n in ("gate", "up", "down"))
    bg, bu, bd = (given[f"L0_cond_B_{n}"][0] for n in ("gate", "up", "down"))
    n_adapters = ag.shape[0]
    a_gu = np.stack([by_partition(ag), by_partition(au)], axis=2)
    a_all = np.concatenate([a_gu.reshape(n_adapters, P, -1), by_partition(ad).reshape(n_adapters, P, -1)],
                           axis=2)
    b_all = np.concatenate([b.transpose(0, 2, 1) for b in (bg, bu, bd)], axis=2)
    arrays = {
        "x_rows": x.reshape(tiles, P, hidden),
        "x_cols": x.reshape(tiles, P, hc, P).transpose(0, 3, 2, 1),
        "w_gu": np.stack([w.T.reshape(hc, P, f) for w in (wg, wu)]),
        "w_down": np.pad(wd.T, ((0, fc * P - f), (0, 0))).reshape(fc, P, hidden),
        "a_all": a_all,
        "b_all": b_all,
        "w_mix": given["L1_cond_weights"],
        "indices": np.stack([given["itok_B_2_6"], given["itok_B_0_15"]])[None],
    }
    arrays = {k: np.ascontiguousarray(v) for k, v in arrays.items()}
    nc = bacc.Bacc("TRN2", target_bir_lowering=False, num_devices=1, dynamic_dma_scratch_size=1024)
    args = [nc.dram_tensor(f"in_{k}", v.shape, mybir.dt.from_np(v.dtype), kind="ExternalInput").ap()
            for k, v in arrays.items()]
    out = nc.dram_tensor("out_0", (tiles, P, hidden), F32, kind="ExternalOutput").ap()
    build(nc, *args, out)
    r = run_bass_kernel_spmd(nc, [{f"in_{k}": v for k, v in arrays.items()}], core_ids=[0])
    return r.results[0]["out_0"].reshape(x.shape)
```
